# Optimizing a Trainium2 kernel written in Bass

```python
import numpy as np
import jax
import jax.numpy as jnp

def _softmax(x, axis=-1):
    return jax.nn.softmax(x, axis=axis)

def _gelu(x):
    return jax.nn.gelu(x, approximate=True)

def _silu(x):
    return jax.nn.silu(x)

def _sigmoid(x):
    return jax.nn.sigmoid(x)

def _layernorm(x, axis=-1, eps=1e-05):
    m = jnp.mean(x, axis=axis, keepdims=True)
    v = jnp.var(x, axis=axis, keepdims=True)
    return (x - m) / jnp.sqrt(v + eps)

def _scatter_add(tgt, idx, src, axis=0):
    return tgt.at[idx].add(src)

def _segment_sum(src, seg, n):
    return jax.ops.segment_sum(src, seg, n)
kernel_name = 'mk_adj_resnorm_d4_adj_r2_6e776f'

def setup_inputs(seed: int=0):
    np.random.seed(seed)
    _w = jnp.asarray

    def _rec_inputs():
        import jax
        import jax.numpy as jnp
        _gk = jax.random.key(seed)
        x = -0.000929 + 1 * jax.random.normal(jax.random.fold_in(_gk, 1), (4096, 128), jnp.float32)
        _a = jax.random.bernoulli(jax.random.fold_in(_gk, 2), 0.000488281, (4096, 4096))
        _a = jnp.logical_or(_a, jnp.swapaxes(_a, -1, -2))
        _a = jnp.logical_or(_a, jnp.eye(4096, dtype=bool))
        _af = _a.astype(jnp.float32)
        adj = _af
        return (x, adj)
    x, adj = _rec_inputs()

    def _L0_gnn_setup():
        import jax, jax.numpy as jnp
        import numpy as np
        N, C_IN, C_OUT = (4096, 128, 128)
        BN_EPS = 1e-05
        EDGE_PROB = 0.004
        key = jax.random.key(seed)
        k1, k2, k3, k4, k5, k6 = jax.random.split(key, 6)
        node_features = jax.random.normal(k1, (N, C_IN), dtype=jnp.float32)
        adjacency_matrix = (jax.random.uniform(k2, (N, N)) < EDGE_PROB).astype(jnp.float32)
        s = 1.0 / np.sqrt(C_IN)
        W_n = jax.random.uniform(k3, (C_OUT, C_IN), jnp.float32, -s, s)
        b_n = jax.random.uniform(k4, (C_OUT,), jnp.float32, -s, s)
        W_c = jax.random.uniform(k5, (C_OUT, C_IN), jnp.float32, -s, s)
        b_c = jax.random.uniform(k6, (C_OUT,), jnp.float32, -s, s)
        gamma = jnp.ones((C_OUT,), jnp.float32)
        beta = jnp.zeros((C_OUT,), jnp.float32)
        return {'node_features': node_features, 'adjacency_matrix': adjacency_matrix, 'W_n': W_n, 'b_n': b_n, 'W_c': W_c, 'b_c': b_c, 'gamma': gamma, 'beta': beta}
    _L0_gnn_all = _L0_gnn_setup()
    _L0_gnn_in = {k: v for k, v in _L0_gnn_all.items() if k in ('W_n', 'b_n', 'W_c', 'b_c', 'gamma', 'beta')}
    del _L0_gnn_all

    def _L1_gnn_setup():
        import jax, jax.numpy as jnp
        import numpy as np
        N = 8192
        F_IN = 128
        F_OUT = 128
        K = 3
        key = jax.random.key(seed)
        k1, k2, k3 = jax.random.split(key, 3)
        x = jax.random.normal(k1, (N, F_IN), dtype=jnp.float32)
        L_tilde = jax.random.normal(k2, (N, N), dtype=jnp.float32) / jnp.sqrt(jnp.float32(N))
        weight = jax.random.normal(k3, (K, F_IN, F_OUT), dtype=jnp.float32) * (1.0 / np.sqrt(F_IN))
        bias = jnp.zeros((F_OUT,), dtype=jnp.float32)
        return {'x': x, 'L_tilde': L_tilde, 'weight': weight, 'bias': bias}
    _L1_gnn_all = _L1_gnn_setup()
    _L1_gnn_in = {k: v for k, v in _L1_gnn_all.items() if k in ('weight', 'bias')}
    del _L1_gnn_all

    def _L2_gnn_setup():
        import jax, jax.numpy as jnp
        import numpy as np
        N = 4096
        D = 128
        EPS = 1e-07
        NEG = -1000000000.0
        key = jax.random.key(seed)
        kx, ka, kb = jax.random.split(key, 3)
        x = jax.random.normal(kx, (N, D), dtype=jnp.float32)
        adj = jax.random.randint(ka, (N, N), 0, 2).astype(jnp.float32)
        adj = adj.at[jnp.arange(N), jnp.arange(N)].set(1.0)
        beta = jax.random.uniform(kb, (1,), dtype=jnp.float32)
        return {'x': x, 'adj': adj, 'beta': beta}
    _L2_gnn_all = _L2_gnn_setup()
    _L2_gnn_in = {k: v for k, v in _L2_gnn_all.items() if k in ('beta',)}
    del _L2_gnn_all

    def _L3_gnn_setup():
        import jax, jax.numpy as jnp
        import numpy as np
        N = 4096
        IN_DIM = 128
        OUT_DIM = 128
        DENSITY = 0.01
        key = jax.random.key(seed)
        kx, ka, kw, ks, kd = jax.random.split(key, 5)
        x = jax.random.normal(kx, (N, IN_DIM), dtype=jnp.float32) * 0.1
        adj_matrix = (jax.random.uniform(ka, (N, N)) < DENSITY).astype(jnp.float32)
        adj_matrix = jnp.maximum(adj_matrix, jnp.eye(N, dtype=jnp.float32))
        weight = jax.random.normal(kw, (OUT_DIM, IN_DIM), dtype=jnp.float32) * 0.05
        att_src = jax.random.normal(ks, (1, OUT_DIM), dtype=jnp.float32) * 0.1
        att_dst = jax.random.normal(kd, (1, OUT_DIM), dtype=jnp.float32) * 0.1
        return {'x': x, 'adj_matrix': adj_matrix, 'weight': weight, 'att_src': att_src, 'att_dst': att_dst}
    _L3_gnn_all = _L3_gnn_setup()
    _L3_gnn_in = {k: v for k, v in _L3_gnn_all.items() if k in ('weight', 'att_src', 'att_dst')}
    del _L3_gnn_all
    return {'x': x, 'adj': adj, 'L0_gnn_W_n': _L0_gnn_in['W_n'], 'L0_gnn_b_n': _L0_gnn_in['b_n'], 'L0_gnn_W_c': _L0_gnn_in['W_c'], 'L0_gnn_b_c': _L0_gnn_in['b_c'], 'L0_gnn_gamma': _L0_gnn_in['gamma'], 'L0_gnn_beta': _L0_gnn_in['beta'], 'L1_gnn_weight': _L1_gnn_in['weight'], 'L1_gnn_bias': _L1_gnn_in['bias'], 'L2_gnn_beta': _L2_gnn_in['beta'], 'L3_gnn_weight': _L3_gnn_in['weight'], 'L3_gnn_att_src': _L3_gnn_in['att_src'], 'L3_gnn_att_dst': _L3_gnn_in['att_dst']}

def reference(x, adj, L0_gnn_W_n, L0_gnn_b_n, L0_gnn_W_c, L0_gnn_b_c, L0_gnn_gamma, L0_gnn_beta, L1_gnn_weight, L1_gnn_bias, L2_gnn_beta, L3_gnn_weight, L3_gnn_att_src, L3_gnn_att_dst):
    import jax
    import jax.numpy as jnp

    def _L0_gnn_ref(node_features, adjacency_matrix, W_n, b_n, W_c, b_c, gamma, beta):
        import jax, jax.numpy as jnp
        import numpy as np
        N, C_IN, C_OUT = (4096, 128, 128)
        BN_EPS = 1e-05
        EDGE_PROB = 0.004
        deg = adjacency_matrix.sum(axis=1, keepdims=True)
        deg = jnp.where(deg == 0, jnp.ones_like(deg), deg)
        agg = adjacency_matrix.T @ node_features / deg
        h = agg @ W_n.T + b_n + node_features @ W_c.T + b_c
        mu = h.mean(axis=0)
        var = ((h - mu) ** 2).mean(axis=0)
        h_norm = (h - mu) * jax.lax.rsqrt(var + BN_EPS)
        return jax.nn.relu(gamma * h_norm + beta)

    def _L1_gnn_ref(x, L_tilde, weight, bias):
        import jax, jax.numpy as jnp
        import numpy as np
        N = 8192
        F_IN = 128
        F_OUT = 128
        K = 3
        T_prev = x
        T_curr = L_tilde @ x
        out = T_prev @ weight[0]
        if K > 1:
            out = out + T_curr @ weight[1]
        for k in range(2, K):
            T_next = 2.0 * (L_tilde @ T_curr) - T_prev
            out = out + T_next @ weight[k]
            T_prev, T_curr = (T_curr, T_next)
        return out + bias

    def _L2_gnn_ref(x, adj, beta):
        import jax, jax.numpy as jnp
        import numpy as np
        N = 4096
        D = 128
        EPS = 1e-07
        NEG = -1000000000.0
        norm2 = jnp.linalg.norm(x, axis=1, keepdims=True)
        cos = beta * (x @ x.T) / (norm2 @ norm2.T + EPS)
        masked = cos + (1.0 - adj) * NEG
        P = jax.nn.softmax(masked, axis=1)
        return P @ x

    def _L3_gnn_ref(x, adj_matrix, weight, att_src, att_dst):
        import jax, jax.numpy as jnp
        import numpy as np
        N = 4096
        IN_DIM = 128
        OUT_DIM = 128
        DENSITY = 0.01
        H = x @ weight.T
        alpha_src = jnp.sum(H * att_src[0], axis=-1)
        alpha_dst = jnp.sum(H * att_dst[0], axis=-1)
        C = alpha_src[None, :] + alpha_dst[:, None]
        Tau = adj_matrix.T * jnp.exp(jnp.maximum(0.2 * C, C))
        att_weights = Tau / jnp.sum(Tau, axis=1, keepdims=True)
        Z = adj_matrix.T * att_weights @ H
        return Z
    x = _layernorm(x + _L0_gnn_ref(x, adj, L0_gnn_W_n, L0_gnn_b_n, L0_gnn_W_c, L0_gnn_b_c, L0_gnn_gamma, L0_gnn_beta), axis=-1)
    x = _layernorm(x + _L1_gnn_ref(x, adj, L1_gnn_weight, L1_gnn_bias), axis=-1)
    x = _layernorm(x + _L2_gnn_ref(x, adj, L2_gnn_beta), axis=-1)
    x = _layernorm(x + _L3_gnn_ref(x, adj, L3_gnn_weight, L3_gnn_att_src, L3_gnn_att_dst), axis=-1)
    return x

_drawn_inputs = setup_inputs


def setup_inputs(seed=0):
    import zlib

    import numpy as np

    out = dict(_drawn_inputs(seed))
    spreads = {'L0_gnn_gamma': (1.0, 0.2), 'L0_gnn_beta': (0.0, 0.1), 'L1_gnn_bias': (0.0, 0.8)}
    factors = {'L0_gnn_b_n': 8.0, 'L0_gnn_b_c': 8.0, 'L3_gnn_att_dst': 2.928}
    for name, (base, spread) in spreads.items():
        noise = np.random.default_rng([zlib.crc32(name.encode()), seed]).standard_normal(out[name].shape)
        drawn = base * np.exp(spread * noise) if base else spread * noise
        out[name] = jnp.asarray(drawn.astype(out[name].dtype))
    for name, factor in factors.items():
        out[name] = (out[name] * factor).astype(out[name].dtype)
    return out
```

```python
from contextlib import ExitStack

import concourse.bass as bass
from concourse import mybir

F32 = mybir.dt.float32
F16 = mybir.dt.float16
F8 = mybir.dt.float8e5
U16 = mybir.dt.uint16
U8 = mybir.dt.uint8
ALU = mybir.AluOpType
ACT = mybir.ActivationFunctionType
AX_X = mybir.AxisListType.X

P = 128
N = 4096
D = 128
NT = N // P
BT = 4
NB = NT // BT
BW = BT * P
NK = NT // 2
HK = NK // 2
LN_EPS = 1e-5
COS_EPS = 1e-7
ONE8 = 60
X0_SCALE = 16.0
S = 4096.0
HS = 256.0
PARTS = 2 * D + 1
UW = D + 1
KB = 1024


class Lap:

    def __init__(self, sem, per=0, base=0):
        self.sem, self.per, self.base, self.round, self.n = sem, per, base, 0, 0

    def start(self, r):
        self.round, self.n = r, 0

    def done(self, ins):
        ins.then_inc(self.sem, 1)
        self.n += 1

    def wait(self, eng):
        eng.wait_ge(self.sem, self.round * self.per + (self.base + self.n))

    def step(self, eng, ins):
        self.done(ins)
        self.wait(eng)


def program(nc, x, adj, wnT, wcT, bn, bc, gamma, beta, w1, b1, cos_beta, w3, w3T, att, out):
    adj_rows = adj.rearrange("(r k p b) c -> r k b p c", r=NB, k=2, b=2)
    adj_casts = adj.rearrange("(k p b) (i c) -> i b p k c", p=P, b=2, c=BW)
    x_nodes = x.rearrange("(k p b) d -> p k (b d)", p=P, b=2)
    out_nodes = out.rearrange("(r k p b) d -> r p k (b d)", r=NB, k=2, b=2)
    a8_dram = nc.dram_tensor("a8_dram", (P, NB * NT, BW), F8).ap()
    a8_blocks = a8_dram.rearrange("p (i k b) c -> i b p k c", i=NB, b=2)
    a8_strips = a8_dram.rearrange("p (s t) c -> s p (t c)", t=8)
    x3_dram = nc.dram_tensor("x3_dram", (P, NT * D), F32).ap()

    with ExitStack() as ctx:
        def sb(name, shape, dt):
            return ctx.enter_context(nc.sbuf_tensor(name, shape, dt))

        def sem(name):
            return ctx.enter_context(nc.semaphore(name))

        def sems(name, n):
            return [sem(f"{name}{i}") for i in range(n)]

        at = sb("at", [P, NB * NK * BW * 2], U8)
        work = sb("work", [P, 73984], U8)
        ident = sb("ident", [P, P], F32)
        ident16 = sb("ident16", [P, P], F16)
        weights = sb("weights", [P, 5, D], F32)
        small = sb("small", [P, 280], F32)

        ps = ctx.enter_context(nc.psum_tensor("ps", [P, 8, 512], F32))

        def view(a, n, dt):
            return work[:, a:a + n].bitcast(dt)

        LD0, NAT0, XP0, AGG0 = 0, 32 * KB, 40 * KB, 40 * KB + NT * PARTS * 2 + 64
        rows = [view(LD0 + 8 * KB * s, 8 * KB, F32) for s in range(4)]
        rows8 = [view(NAT0 + 2 * KB * s, 2 * KB, F8) for s in range(4)]
        xp = view(XP0, NT * PARTS * 2, F16).rearrange("p (t c) -> p t c", t=NT)
        aggT = view(AGG0, 16 * KB, F32)
        xn = view(0, 16 * KB, F32).rearrange("p (t d) -> p t d", t=NT)
        x1T = view(16 * KB, 16 * KB, F32)
        ring = [view(4 * KB * c, 4 * KB, F8) for c in range(4)]
        vp = view(AGG0, 16 * KB, F16).rearrange("p (t c) -> p t c", t=NT)
        tmp = [view(NAT0 + 2 * KB * s, 2 * KB, F32) for s in range(4)]
        yT = view(16 * KB, 16 * KB, F16).rearrange("p (r h i) -> p r h i", r=NB, h=2)
        small_n = [0]

        def col(n=1):
            a = small_n[0]
            small_n[0] += n
            return small[:, a:a + n]

        bnc, bcc, hbias, gam, bet, b1c, cosb, cscale, cbias = [col() for _ in range(9)]
        deg4 = col(4)
        degp = col(2 * NT)
        rdeg = col(NT)
        eq0 = col(NT)
        bstat = col(NB * 6)
        bagg, bscale, btmp = col(2), col(), col()
        stat4 = col(BT * 6).rearrange("p (t c) -> p t c", t=BT)
        mv4 = col(BT * 2).rearrange("p (t c) -> p t c", t=BT)
        va4, rs4, half4, n24, rn4, va4b, s4, eps4, epss4, epsc4 = [col(BT) for _ in range(10)]
        w_1, w_2, w_b, wn_s, wc_s = [weights[:, j, :] for j in range(5)]

        LAG = 3
        expo = [view(4 * KB * j, 4 * KB, F32) for j in range(4)]
        ehigh = [view(AGG0 + 4 * KB * j, 2 * KB, F16) for j in range(4)]
        elow = [view(AGG0 + 4 * KB * j + 2 * KB, 2 * KB, F16) for j in range(4)]
        psum_kept = view(NAT0, BT * PARTS * 4, F32).rearrange("p (s c) -> p s c", s=BT)
        res4 = view(NAT0 + BT * PARTS * 4 + 16, BT * D * 4, F32).rearrange("p (s d) -> p s d", s=BT)
        place = [0]

        def late(n, dt, size):
            a = place[0]
            place[0] += (n * size + 31) // 32 * 32
            return at[:, a:a + n * size].bitcast(dt)

        x3n = late(NT * D, F32, 4).rearrange("p (t d) -> p t d", t=NT)
        x3T = late(N, F32, 4)
        t_row = late(N, F32, 4)
        hx = late(NT * UW, F32, 4).rearrange("p (t c) -> p t c", t=NT)
        ug = [late(NT * 2 * UW, F16, 2).rearrange("p (t c) -> p t c", t=NT) for _ in range(2)]
        uf = [late(BT * UW, F32, 4).rearrange("p (t c) -> p t c", t=BT) for _ in range(2)]
        zs = late(8 * 2 * UW, F32, 4).rearrange("p (j c) -> p j c", j=8)
        w3s, w3Ts, vrow = late(D, F32, 4), late(D, F32, 4), late(D, F32, 4)
        atts, vst, st = late(2, F32, 4), late(2, F32, 4), late(2 * NT, F32, 4).rearrange("p (t c) -> p t c", t=NT)
        neg_s, wt1, wt2, rr = late(NT, F32, 4), late(NT, F32, 4), late(NT, F32, 4), late(NT, F32, 4)
        mx, mxrow, mall, ones_row = late(1, F32, 4), late(1, F32, 4), late(4, F32, 4), late(P, F32, 4)
        den4 = late(BT, F32, 4)
        assert place[0] <= 128 * KB
        a8ring = [view(4 * KB * c, 4 * KB, U8) for c in range(4)]
        code = [view(16 * KB + 2 * KB * j, 2 * KB, F16) for j in range(4)]
        gate = [[view((24 + 8 * g) * KB + 2 * KB * j, 2 * KB, F16) for j in range(4)] for g in range(2)]
        outs = view(40 * KB, BT * D * 4, F32).rearrange("p (s d) -> p s d", s=BT)

        const_in, const_ready = sem("const_in"), sem("const_ready")
        x_in, row_in = sem("x_in"), sems("row_in", 4)
        x_high, x_low = sem("x_high"), sem("x_low")
        row_cast, deg_kept, xs_copied = sems("row_cast", 4), sems("deg_kept", 4), sems("xs_copied", 4)
        row_used, at_ps, at_written = sems("row_used", 4), sems("at_ps", 4), sems("at_written", 2)
        agg_ps, agg_kept = sem("agg_ps"), sem("agg_kept")
        dve_lap, pool_lap, act_lap = sem("dve_lap"), sem("pool_lap"), sem("act_lap")
        xn_in, xt_ps, xt_kept = sem("xn_in"), sem("xt_ps"), sem("xt_kept")
        rdeg_ready, rb_ps, agg_scaled = sem("rdeg_ready"), sem("rb_ps"), sem("agg_scaled")
        h_ps, h_kept, h_norm, h_relu = sem("h_ps"), sem("h_kept"), sem("h_norm"), sem("h_relu")
        bvar_ready, brstd_ready = sem("bvar_ready"), sem("brstd_ready")
        r_ps, z_ready, var_ready, rstd_ready = sem("r_ps"), sem("z_ready"), sem("var_ready"), sem("rstd_ready")
        xs_ready, x1_high, x1_low, x1t_ps, x1t_kept = (sem("xs_ready"), sem("x1_high"), sem("x1_low"),
                                                       sem("x1t_ps"), sem("x1t_kept"))
        ring_in, strip_used = sems("ring_in", 4), sems("strip_used", 3)
        prod_ps, prod_kept = sem("prod_ps"), sem("prod_kept")
        ring_done = strip_used + [prod_ps]
        vt_ps, vt_kept, vn_ps, vn_kept = sem("vt_ps"), sem("vt_kept"), sem("vn_ps"), sem("vn_kept")
        o_ps, x2s_ready, x2_high, x2_low = sem("o_ps"), sem("x2s_ready"), sem("x2_high"), sem("x2_low")
        sq_ready, rn_ready, y_ready, y_ps = sem("sq_ready"), sem("rn_ready"), sem("y_ready"), sem("y_ps")
        y_high, y_kept, a8_out = sem("y_high"), sem("y_kept"), sems("a8_out", 4)
        s_ps, exp_ready, mask_ready = sems("s_ps", 2), sems("exp_ready", 2), sem("mask_ready")
        high_ready, low_ready, pv_done = sem("high_ready"), sems("low_ready", 4), sems("pv_done", 4)
        pv_kept, num_ready, res_ready, res_norm, x3_out = (sem("pv_kept"), sem("num_ready"), sem("res_ready"),
                                                           sem("res_norm"), sem("x3_out"))
        w3_in, x3_in, l3_lap = sem("w3_in"), sem("x3_in"), sem("l3_lap")
        v_ps, v_ready, x3t_ps, x3t_kept, hst_ps, t_ps = (sem("v_ps"), sem("v_ready"), sem("x3t_ps"), sem("x3t_kept"),
                                                         sem("hst_ps"), sem("t_ps"))
        h_out, st_out, t_out, mx_ps, mall_ready, w_ready = (sem("h_out"), sem("st_out"), sem("t_out"), sem("mx_ps"),
                                                            sem("mall_ready"), sem("w_ready"))
        uf_ready, u_high, u_low = sem("uf_ready"), sem("u_high"), sem("u_low")
        a8_in, code_ready, g1_ready, g2_ready = sems("a8_in", 4), sem("code_ready"), sem("g1_ready"), sem("g2_ready")
        gates_used, z_ps, z_kept, z_sum = sems("gates_used", 4), sem("z_ps"), sem("z_kept"), sem("z_sum")
        zz_ready, out_ready, mx_ready = sem("zz_ready"), sem("out_ready"), sem("mx_ready")
        xs_tile = sb("xs_tile", [P, 4, 2, D], F16)
        zero16 = sb("zero16", [P, P], F16)
        done = sem("done")

        block = ctx.enter_context(nc.Block())

        def node_block(v, r):
            return v[:, r * BT:(r + 1) * BT, :]

        def gate_free(eng, r, k, first):
            if k % 4 < 3:
                eng.wait_ge(gates_used[k % 4], r * 4 + k // 4)
            elif k > 3:
                eng.wait_ge(gates_used[3], r * 3 + k // 4)
            elif not first:
                eng.wait_ge(z_ps, r * 8)

        @block.sync
        def _(sp):
            sp.dma_start(aggT.rearrange("p (k c) -> p k c", k=NK), x_nodes).then_inc(x_in, 16)
            for h in range(2):
                with sp.Fori(0, NB) as g:
                    for s in range(4):
                        sp.wait_ge(row_cast[s], g + h * NB)
                        sp.dma_start(rows[s], adj_rows[bass.ds(g, 1), s // 2, s % 2, :, h * 2048:(h + 1) * 2048]
                                     .rearrange("r p c -> (r p) c")).then_inc(row_in[s], 16)
            for s in range(4):
                sp.wait_ge(row_cast[s], 2 * NB)
            sp.dma_start(xn.rearrange("p (k b) d -> p k (b d)", b=2), x_nodes).then_inc(xn_in, 16)
            for n in range(2):
                if n == 0:
                    for c in range(4):
                        for q in (x1_low, x1_high, x1t_ps):
                            sp.wait_ge(q, 2 * c + 2)
                with sp.Fori(0, NB) as r:
                    for c in range(4):
                        sp.wait_ge(ring_done[c], r + n * NB)
                        sp.dma_start(ring[c].bitcast(U8), at[:, bass.ds((r * 4 + c) * (4 * KB), 4 * KB)]
                                     ).then_inc(ring_in[c], 16)
            with sp.Fori(0, NB) as r:
                sp.wait_ge(res_norm, r + 1)
                sp.dma_start(x3_dram[:, bass.ds(r * (BT * D), BT * D)], res4.rearrange("p s d -> p (s d)")
                             ).then_inc(x3_out, 16)
            sp.wait_ge(mask_ready, NB * NK)
            sp.wait_ge(x3_out, 16 * NB)
            sp.dma_start(x3n.rearrange("p t d -> p (t d)"), x3_dram).then_inc(x3_in, 16)
            sp.dma_start(w3s, w3).then_inc(w3_in, 16)
            sp.dma_start(w3Ts, w3T).then_inc(w3_in, 16)
            sp.dma_start(atts, att).then_inc(w3_in, 16)
            for q in a8_out:
                sp.wait_ge(q, 16 * 2 * NB // 4)
            for j in range(4):
                sp.wait_ge(low_ready[j], NB * 4)
            for r in range(NB + 2):
                for c in range(4 if r < NB else 0):
                    if r:
                        sp.wait_ge(code_ready, r * NK + (4 * c + 4 - NK))
                    sp.dma_start(a8ring[c], a8_strips[r * 4 + c].bitcast(U8)).then_inc(a8_in[c], 16)
                if r >= 2:
                    sp.wait_ge(out_ready, r - 1)
                    sp.dma_start(out_nodes[r - 2], outs.rearrange("p (k b) d -> p k (b d)", k=2)
                                 ).then_inc(done, 16)
            sp.wait_ge(done, 16 * NB)

        @block.gpsimd
        def _(pool):
            lap = Lap(pool_lap)
            lap.step(pool, pool.memset(ident[:, :], 0.0))
            lap.step(pool, pool.affine_select(out=ident[:, :], in_=ident[:, :], compare_op=ALU.not_equal, fill=1.0,
                                              base=0, pattern=[[-1, P]], channel_multiplier=1))
            pool.tensor_copy(ident16[:, :], ident[:, :])
            pool.memset(zero16[:, :], 0.0)
            for dst, value in ((s4, S), (eps4, LN_EPS), (epss4, LN_EPS * S * S), (epsc4, COS_EPS)):
                pool.memset(dst, value)
            pool.memset(half4, -0.5).then_inc(const_ready, 1)

            def inverse_root(dst, value, eps, signal, scale=None):
                lap.step(pool, pool.tensor_tensor(va4, value, eps, ALU.add))
                if scale is None:
                    pool.tensor_tensor(dst, va4, half4, ALU.pow).then_inc(signal, 1)
                else:
                    lap.step(pool, pool.tensor_tensor(dst, va4, half4, ALU.pow))
                    pool.tensor_tensor(dst, dst, scale, ALU.mult).then_inc(signal, 1)

            pool.wait_ge(x_low, 4)
            pool.wait_ge(x_high, 4)
            for h in range(2):
                with pool.Fori(0, NB) as g:
                    for s in range(4):
                        pool.wait_ge(row_used[s], g + h * NB)
                        pool.tensor_copy(xs_tile[:, s, :, :].rearrange("p h d -> p (h d)"),
                                         xp[:, bass.ds(g * BT + s, 1), 0:2 * D].rearrange("p t c -> p (t c)")
                                         ).then_inc(xs_copied[s], 1)
                        pool.wait_ge(row_cast[s], g + (h * NB + 1))
                        pool.tensor_copy(degp[:, bass.ds(g * BT + (h * NT + s), 1)], deg4[:, s:s + 1]
                                         ).then_inc(deg_kept[s], 1)
            pool.wait_ge(bvar_ready, 1)
            lap.step(pool, pool.tensor_scalar(bscale, bagg[:, 1:2], LN_EPS, None, ALU.add))
            lap.step(pool, pool.tensor_tensor(bscale, bscale, half4[:, 0:1], ALU.pow))
            pool.tensor_tensor(bscale, bscale, gam, ALU.mult).then_inc(brstd_ready, 1)
            for r in range(NB):
                pool.wait_ge(var_ready, r + 1)
                inverse_root(rs4, mv4[:, :, 1], eps4, rstd_ready, s4)

            pool.wait_ge(z_ready, NB)
            for r in range(2 * NB):
                i, b = r // 2, r % 2
                if r >= 4:
                    pool.wait_ge(a8_out[r % 4], 16 * (r // 4))
                pool.dma_start(a8_blocks[i, b], adj_casts[i, b]
                               ).then_inc(a8_out[r % 4], 16)
                if r < NB:
                    continue
                q = r - NB
                pool.wait_ge(var_ready, NB + q + 1)
                inverse_root(rs4, mv4[:, :, 1], eps4, rstd_ready, s4)
                pool.wait_ge(sq_ready, q + 1)
                inverse_root(rn4, n24, epsc4, rn_ready)
            lap.per, lap.base = 3, lap.n
            with pool.Fori(0, NB) as r:
                lap.start(r)
                pool.wait_ge(pv_kept, r * BT + BT)
                pool.wait_ge(x3_out, r * 16)
                lap.step(pool, pool.tensor_tensor(psum_kept[:, :, D:2 * D], psum_kept[:, :, 0:D],
                                                  psum_kept[:, :, D:2 * D], ALU.add))
                blk = xp[:, bass.ds(r * BT, BT), :]
                pool.tensor_tensor(res4, blk[:, :, 0:D], blk[:, :, D:2 * D], ALU.add).then_inc(num_ready, 1)
                pool.wait_ge(var_ready, r + (2 * NB + 1))
                inverse_root(rs4, mv4[:, :, 1], epss4, rstd_ready, s4)
            lap.base += 3 * NB
            lap.per = 1
            with pool.Fori(0, NB) as r:
                lap.start(r)
                pool.wait_ge(z_kept, r * 8 + 8)
                pool.tensor_tensor(zs[:, :, 0:UW], zs[:, :, 0:UW], zs[:, :, UW:2 * UW], ALU.add).then_inc(z_sum, 1)
                pool.wait_ge(var_ready, r + (3 * NB + 1))
                inverse_root(rs4, mv4[:, :, 1], epss4, rstd_ready)

        @block.scalar
        def _(act):
            for dst, src in ((wn_s, wnT), (wc_s, wcT), (w_1, w1[1]), (w_2, w1[2]), (w_b, w1[0])):
                act.dma_start(dst, src).then_inc(const_in, 16)
            for dst, src in ((bnc, bn), (bcc, bc), (gam, gamma), (bet, beta), (b1c, b1)):
                act.dma_start(dst, src.rearrange("(p o) -> p o", o=1)).then_inc(const_in, 16)
            act.dma_start(cosb, cos_beta.rearrange("(p o) -> p o", o=1).to_broadcast([P, 1])).then_inc(const_in, 16)
            act.wait_ge(x_in, 16)
            xf = aggT.rearrange("p (t d) -> p t d", t=NT)
            for c in range(4):
                act.activation(xp[:, c * 8:(c + 1) * 8, D:2 * D], xf[:, c * 8:(c + 1) * 8, :], ACT.Copy,
                               scale=X0_SCALE).then_inc(x_high, 1)
            for h in range(2):
                with act.Fori(0, NB) as g:
                    for s in range(4):
                        act.wait_ge(row_in[s], g * 16 + (h * NB + 1) * 16)
                        act.wait_ge(row_used[s], g + h * NB)
                        act.wait_ge(deg_kept[s], g + h * NB)
                        act.activation(rows8[s].bitcast(U8), rows[s], ACT.Copy, scale=float(ONE8),
                                       accum_out=deg4[:, s:s + 1]).then_inc(row_cast[s], 1)
            for r in range(NB):
                act.wait_ge(xt_ps, r + 1)
                act.copy(x1T[:, r * BW:(r + 1) * BW], ps[:, r % 2, :]).then_inc(xt_kept, 1)
            for r in range(NB):
                hb = aggT[:, r * BW:(r + 1) * BW]
                act.wait_ge(h_ps, r + 1)
                act.activation(hb, ps[:, 4 + r % 2, :], ACT.Identity, bias=hbias).then_inc(h_kept, 1)

            def high_and_transposed(r):
                act.wait_ge(xs_ready, r + 1)
                act.copy(node_block(xp, r)[:, :, D:2 * D], node_block(xn, r)).then_inc(x1_high, 1)
                act.wait_ge(x1t_ps, r + 1)
                act.copy(x1T[:, r * BW:(r + 1) * BW], ps[:, r % 2, :]).then_inc(x1t_kept, 1)

            for r in range(NB):
                hb = aggT[:, r * BW:(r + 1) * BW]
                act.wait_ge(h_norm, r + 1)
                act.activation(hb, hb, ACT.Relu, bias=bet).then_inc(h_relu, 1)
                if r:
                    high_and_transposed(r - 1)
            high_and_transposed(NB - 1)

            with act.Fori(0, NB) as r:
                act.wait_ge(prod_ps, r + 1)
                act.wait_ge(vt_ps, r)
                act.mul(tmp[0], ps[:, 0, :], 1.0 / S).then_inc(prod_kept, 1)
                act.wait_ge(vt_ps, r + 1)
                act.wait_ge(vn_ps, r)
                act.copy(tmp[1], ps[:, 1, :]).then_inc(vt_kept, 1)
            with act.Fori(0, NB) as r:
                act.wait_ge(prod_ps, r + (NB + 1))
                act.wait_ge(o_ps, r)
                act.activation(tmp[0], ps[:, 0, :], ACT.Identity, bias=b1c).then_inc(prod_kept, 1)
                act.wait_ge(x2s_ready, r + 1)
                x2s = tmp[1].rearrange("p (t d) -> p t d", t=BT)
                act.copy(xp[:, bass.ds(r * BT, BT), D:2 * D], x2s).then_inc(x2_high, 1)
                for s in range(BT):
                    last = act.activation(tmp[3][:, s * D:(s + 1) * D], x2s[:, s, :], ACT.Square, scale=1.0 / S,
                                          accum_out=n24[:, s:s + 1])
                last.then_inc(sq_ready, 1)
                act.wait_ge(y_ps, r + 1)
                act.copy(yT[:, bass.ds(r, 1), 0, :].rearrange("p r i -> p (r i)"), ps[:, 2, :]).then_inc(y_high, 1)

            def exponentials(r, k, first):
                act.wait_ge(s_ps[k % 2], r * (NK // 2) + (k // 2 + 1))
                if not (first and k < 4):
                    act.wait_ge(low_ready[k % 4], r * 4 + k // 4)
                act.activation(expo[k % 4], ps[:, 4 + 2 * (k % 2):6 + 2 * (k % 2), :].rearrange("p b i -> p (b i)"),
                               ACT.Exp, bias=cbias, scale=cscale).then_inc(exp_ready[k % 2], 1)

            def exp_high(r, k):
                act.wait_ge(mask_ready, r * NK + (k + 1))
                act.wait_ge(pv_done[k % 4], r * 4 + k // 4)
                act.copy(ehigh[k % 4], expo[k % 4]).then_inc(high_ready, 1)

            def keep_sums(r):
                act.wait_ge(pv_done[(NK - 1) % 4], r * 4 + 4)
                act.wait_ge(res_ready, r)
                for s in range(BT):
                    act.copy(psum_kept[:, s, :], ps[:, s, 0:PARTS]).then_inc(pv_kept, 1)

            def attention_round(r, first):
                for k in range(NK):
                    if k == LAG and not first:
                        keep_sums(r - 1)
                    exponentials(r, k, first)
                    if k:
                        exp_high(r, k - 1)
                    elif not first:
                        exp_high(r - 1, NK - 1)

            attention_round(0, True)
            with act.Fori(1, NB) as r:
                attention_round(r, False)
            exp_high(NB - 1, NK - 1)
            keep_sums(NB - 1)

            for r in range(NB):
                act.wait_ge(x3t_ps, r + 1)
                act.copy(x3T[:, r * BW:(r + 1) * BW], ps[:, r % 2, :]).then_inc(x3t_kept, 1)
                act.wait_ge(hst_ps, r + 1)
                act.copy(node_block(st, r).rearrange("p t c -> p (t c)"), ps[:, 4 + r % 2, 0:2 * BT]
                         ).then_inc(st_out, 1)
                act.wait_ge(t_ps, r + 1)
                act.copy(t_row[:, r * BW:(r + 1) * BW].rearrange("p (k q b) -> p k b q", k=2, b=2),
                         ps[:, 6 + r % 2, :].rearrange("p (k b q) -> p k b q", k=2, b=2)).then_inc(t_out, 1)
            act.wait_ge(mall_ready, 1)
            act.wait_ge(st_out, NB)
            act.activation(wt1, st[:, :, 0], ACT.Exp, bias=mall[:, 1:2])
            act.activation(wt2, st[:, :, 0], ACT.Exp, bias=mall[:, 2:3], scale=0.2).then_inc(w_ready, 1)
            act.activation(rr, st[:, :, 1], ACT.Exp, bias=mall[:, 3:4], scale=0.8).then_inc(w_ready, 1)
            for r in range(NB):
                for g in range(2):
                    act.wait_ge(uf_ready, 2 * r + g + 1)
                    act.copy(node_block(ug[g], r)[:, :, UW:2 * UW], uf[g]).then_inc(u_high, 1)

            def positive(r, k, first):
                act.wait_ge(code_ready, r * NK + (k + 1))
                gate_free(act, r, k, first)
                act.activation(gate[0][k % 4], code[k % 4], ACT.Relu, bias=mall[:, 0:1]).then_inc(g1_ready, 1)

            def keep_z(r):
                for j in range(8):
                    act.wait_ge(z_ps, r * 8 + (j + 1))
                    if j == 0:
                        act.wait_ge(zz_ready, r)
                    act.copy(zs[:, j, :], ps[:, j, 0:2 * UW]).then_inc(z_kept, 1)

            def gat_round(r, first):
                for k in range(NK):
                    if k == 3 and not first:
                        keep_z(r - 1)
                    positive(r, k, first)

            gat_round(0, True)
            with act.Fori(1, NB) as r:
                gat_round(r, False)
            keep_z(NB - 1)

        @block.vector
        def _(dve):
            lap = Lap(dve_lap)
            dve.wait_ge(const_ready, 1)
            dve.wait_ge(const_in, 16 * 11)
            lap.step(dve, dve.tensor_tensor(w_b, w_b, w_2, ALU.subtract))
            lap.step(dve, dve.tensor_tensor(w_b, w_b, ident[:, :], ALU.add))
            dve.tensor_scalar(w_b, w_b, 1.0 / S, None, ALU.mult)
            dve.tensor_scalar(w_1, w_1, 1.0 / S, None, ALU.mult)
            dve.tensor_scalar(w_2, w_2, 2.0, None, ALU.mult)
            dve.tensor_tensor(hbias, bnc, bcc, ALU.add)
            dve.tensor_scalar(cscale, cosb, S ** -2, None, ALU.mult)
            lap.step(dve, dve.tensor_scalar(cbias, cosb, -1.0, None, ALU.mult))
            dve.tensor_tensor(cbias, cosb, cbias, ALU.min).then_inc(const_ready, 1)
            xf = aggT.rearrange("p (t d) -> p t d", t=NT)
            for c in range(4):
                dve.wait_ge(x_high, c + 1)
                dve.scalar_tensor_tensor(xp[:, c * 8:(c + 1) * 8, 0:D], xf[:, c * 8:(c + 1) * 8, :], X0_SCALE,
                                         xp[:, c * 8:(c + 1) * 8, D:2 * D], ALU.mult, ALU.subtract
                                         ).then_inc(x_low, 1)
            at16 = at[:, :].bitcast(U16)
            for h in range(2):
                with dve.Fori(0, NB) as g:
                    for s in range(4):
                        dve.wait_ge(at_ps[s], g + (h * NB + 1))
                        src = ps[:, 4 + s % 2, :].bitcast(U16).rearrange("p (k i) -> p k i", k=HK)
                        dst = at16[:, bass.ds(g * (NK * BW) + h * HK * BW, HK * BW)].rearrange(
                            "p (k i) -> p k i", k=HK)[:, :, s * P:(s + 1) * P]
                        dve.tensor_copy(dst, src).then_inc(at_written[s % 2], 1)
                for j in range(4):
                    dve.wait_ge(agg_ps, 4 * h + j + 1)
                    dve.tensor_copy(aggT[:, h * 2048 + j * BW:h * 2048 + (j + 1) * BW], ps[:, j, :]
                                    ).then_inc(agg_kept, 1)
            for s in range(4):
                dve.wait_ge(deg_kept[s], 2 * NB)
            lap.step(dve, dve.tensor_tensor(rdeg, degp[:, 0:NT], degp[:, NT:2 * NT], ALU.add))
            lap.step(dve, dve.tensor_scalar(eq0, rdeg, 0.0, float(ONE8), ALU.is_equal, ALU.mult))
            lap.step(dve, dve.tensor_tensor(rdeg, rdeg, eq0, ALU.add))
            lap.step(dve, dve.tensor_scalar(rdeg, rdeg, X0_SCALE / ONE8, None, ALU.mult))
            dve.reciprocal(rdeg, rdeg).then_inc(rdeg_ready, 1)
            dve.wait_ge(agg_kept, 8)
            for r in range(NB):
                hb = aggT[:, r * BW:(r + 1) * BW]
                dve.wait_ge(rb_ps, r + 1)
                dve.tensor_tensor(hb, hb, ps[:, 2 + r % 2, :], ALU.mult).then_inc(agg_scaled, 1)
            for r in range(NB):
                dve.wait_ge(h_kept, r + 1)
                last = dve.bn_stats(bstat[:, 6 * r:6 * r + 6], aggT[:, r * BW:(r + 1) * BW])
            lap.step(dve, last)
            dve.bn_aggr(bagg, bstat).then_inc(bvar_ready, 1)
            dve.wait_ge(brstd_ready, 1)
            dve.wait_ge(bvar_ready, 1)
            for r in range(NB):
                hb = aggT[:, r * BW:(r + 1) * BW]
                dve.tensor_scalar(hb, hb, bagg[:, 0:1], bscale, ALU.subtract, ALU.mult).then_inc(h_norm, 1)

            def low(r):
                dve.wait_ge(x1_high, r + 1)
                dve.tensor_tensor(node_block(xp, r)[:, :, 0:D], node_block(xn, r), node_block(xp, r)[:, :, D:2 * D],
                                  ALU.subtract).then_inc(x1_low, 1)

            dve.memset(xp[:, :, 2 * D:PARTS], 1.0)
            dve.wait_ge(xn_in, 16)
            for r in range(NB):
                z = node_block(xn, r)
                dve.wait_ge(r_ps, r + 1)
                dve.wait_ge(xt_ps, NB)
                dve.tensor_tensor(z, z, ps[:, 6 + r % 2, :].rearrange("p (t d) -> p t d", t=BT),
                                  ALU.add).then_inc(z_ready, 1)
                dve.wait_ge(z_ready, r + 1)
                for s in range(BT):
                    last = dve.bn_stats(stat4[:, s, :], z[:, s, :])
                lap.step(dve, last)
                for s in range(BT):
                    last = dve.bn_aggr(mv4[:, s, :], stat4[:, s, :])
                last.then_inc(var_ready, 1)
                if r:
                    low(r - 1)
                dve.wait_ge(var_ready, r + 1)
                dve.wait_ge(rstd_ready, r + 1)
                for s in range(BT):
                    last = dve.tensor_scalar(z[:, s, :], z[:, s, :], mv4[:, s, 0:1], rs4[:, s:s + 1],
                                             ALU.subtract, ALU.mult)
                last.then_inc(xs_ready, 1)
            low(NB - 1)

            lap.per, lap.base = 1, lap.n
            with dve.Fori(0, NB) as r:
                lap.start(r)
                v = vp[:, bass.ds(r * BT, BT), :]
                src = ps[:, 2, :].rearrange("p (t d) -> p t d", t=BT)
                dve.wait_ge(vn_ps, r + 1)
                lap.step(dve, dve.tensor_copy(v[:, :, D:2 * D], src))
                dve.tensor_tensor(v[:, :, 0:D], src, v[:, :, D:2 * D], ALU.subtract).then_inc(vn_kept, 1)

            def moments(z, n):
                for s in range(BT):
                    last = dve.bn_stats(stat4[:, s, :], z[:, s, :])
                lap.step(dve, last)
                dve.memset(btmp, 0.0)
                for s in range(BT):
                    last = dve.bn_aggr(mv4[:, s, :], stat4[:, s, :])
                last.then_inc(var_ready, 1)

            def normed(dst, z, n, signal):
                dve.wait_ge(var_ready, n)
                dve.wait_ge(rstd_ready, n)
                for s in range(BT):
                    last = dve.tensor_scalar(dst[:, s, :], z[:, s, :], mv4[:, s, 0:1], rs4[:, s:s + 1],
                                             ALU.subtract, ALU.mult)
                last.then_inc(signal, 1)

            lap.base += NB
            lap.per = 1
            x2s = tmp[1].rearrange("p (t d) -> p t d", t=BT)
            ys = tmp[2].rearrange("p (t d) -> p t d", t=BT)
            with dve.Fori(0, NB) as r:
                lap.start(r)
                o = ps[:, 1, :].rearrange("p (t d) -> p t d", t=BT)
                dve.wait_ge(o_ps, r + 1)
                moments(o, 0)
                dve.wait_ge(x2_high, r)
                dve.wait_ge(sq_ready, r)
                normed(x2s, o, r + (NB + 1), x2s_ready)
                blk = xp[:, bass.ds(r * BT, BT), :]
                dve.wait_ge(x2_high, r + 1)
                dve.tensor_tensor(blk[:, :, 0:D], x2s, blk[:, :, D:2 * D], ALU.subtract).then_inc(x2_low, 1)
                dve.wait_ge(rn_ready, r + 1)
                dve.wait_ge(y_ps, r)
                for s in range(BT):
                    last = dve.tensor_scalar(ys[:, s, :], x2s[:, s, :], rn4[:, s:s + 1], None, ALU.mult)
                last.then_inc(y_ready, 1)
                dve.wait_ge(y_high, r + 1)
                yb = yT[:, bass.ds(r, 1), :, :].rearrange("p r h i -> p (r h) i")
                dve.tensor_tensor(yb[:, 1, :], ps[:, 2, :], yb[:, 0, :], ALU.subtract).then_inc(y_kept, 1)

            def mask(r, k):
                dve.wait_ge(exp_ready[k % 2], r * (NK // 2) + (k // 2 + 1))
                m = at[:, bass.ds(r * (NK * BW * 2) + k * BW * 2, BW * 2)] if not isinstance(r, int) else \
                    at[:, r * (NK * BW * 2) + k * BW * 2:r * (NK * BW * 2) + (k + 1) * BW * 2]
                e = expo[k % 4].rearrange("p (b i) -> p b i", b=2)
                dve.scalar_tensor_tensor(e, m.rearrange("p (i b) -> p b i", b=2), 0.0, e, ALU.is_gt, ALU.mult
                                         ).then_inc(mask_ready, 1)

            def exp_low(r, k):
                dve.wait_ge(high_ready, r * NK + (k + 1))
                dve.tensor_tensor(elow[k % 4], expo[k % 4], ehigh[k % 4], ALU.subtract).then_inc(low_ready[k % 4], 1)

            def attention_result(r, step):
                if step == 0:
                    dve.wait_ge(num_ready, r + 1)
                    lap.step(dve, dve.reciprocal(va4b, psum_kept[:, :, 2 * D]))
                    for s in range(BT):
                        last = dve.scalar_tensor_tensor(res4[:, s, :], psum_kept[:, s, D:2 * D], va4b[:, s:s + 1],
                                                        res4[:, s, :], ALU.mult, ALU.add)
                    last.then_inc(res_ready, 1)
                if step == 1:
                    dve.wait_ge(res_ready, r + 1)
                    moments(res4, 0)
                if step == 2:
                    normed(res4, res4, r + (2 * NB + 1), res_norm)

            def attention_round(r, first):
                for k in range(NK):
                    mask(r, k)
                    if k:
                        exp_low(r, k - 1)
                    elif not first:
                        exp_low(r - 1, NK - 1)
                    if not first and k in (7, 8, 10):
                        attention_result(r - 1, (7, 8, 10).index(k))

            lap.base += NB
            lap.per = 2
            attention_round(0, True)
            with dve.Fori(1, NB) as r:
                lap.start(r - 1)
                attention_round(r, False)
            exp_low(NB - 1, NK - 1)
            lap.start(NB - 1)
            for step in range(3):
                attention_result(NB - 1, step)
            lap.base += 2 * NB
            lap.per, lap.round, lap.n = 0, 0, 0

            dve.wait_ge(w3_in, 48)
            dve.tensor_scalar(w3Ts, w3Ts, HS / S, None, ALU.mult)
            dve.wait_ge(v_ps, 1)
            lap.step(dve, dve.tensor_scalar(vst, ps[:, 4, 0:2], 1.0 / S, None, ALU.mult))
            dve.tensor_copy(vrow, vst[:, 1:2].to_broadcast([P, P])).then_inc(v_ready, 1)
            dve.memset(hx[:, :, D:UW], HS)
            dve.memset(ones_row[0:1, :], 1.0)
            for r in range(NB):
                dve.wait_ge(hst_ps, r + 1)
                dve.tensor_copy(node_block(hx, r)[:, :, 0:D], ps[:, 2 + r % 2, :].rearrange("p (t d) -> p t d", t=BT)
                                ).then_inc(h_out, 1)
            dve.wait_ge(st_out, NB)
            dve.tensor_scalar(neg_s, st[:, :, 0], -1.0, None, ALU.mult)
            dve.tensor_reduce(mx, st[:, :, 0], AX_X, ALU.max).then_inc(mx_ready, 1)
            dve.wait_ge(mx_ps, 1)
            dve.tensor_reduce(mxrow[0:1, :], ps[0:1, 0, 0:P], AX_X, ALU.max).then_inc(mx_ready, 1)
            dve.wait_ge(mx_ps, 2)
            dve.memset(mall[:, 0:1], -float(ONE8))
            dve.tensor_scalar(mall[:, 1:2], ps[:, 0, 0:1], -1.0, None, ALU.mult)
            dve.tensor_scalar(mall[:, 2:3], ps[:, 0, 0:1], -0.2, None, ALU.mult)
            dve.tensor_scalar(mall[:, 3:4], ps[:, 0, 0:1], 0.8, None, ALU.mult).then_inc(mall_ready, 1)
            dve.wait_ge(w_ready, 1)
            dve.wait_ge(h_out, NB)

            def u_low_part(n):
                r, g = n // 2, n % 2
                dve.wait_ge(u_high, n + 1)
                dve.tensor_tensor(node_block(ug[g], r)[:, :, 0:UW], uf[g], node_block(ug[g], r)[:, :, UW:2 * UW],
                                  ALU.subtract).then_inc(u_low, 1)

            for n in range(2 * NB):
                r, g = n // 2, n % 2
                w = (wt1, wt2)[g][:, r * BT:(r + 1) * BT].rearrange("p (t o) -> p t o", o=1).to_broadcast([P, BT, UW])
                if n >= 2:
                    dve.wait_ge(u_low, n - 1)
                dve.tensor_tensor(uf[g], node_block(hx, r), w, ALU.mult).then_inc(uf_ready, 1)
                if n:
                    u_low_part(n - 1)
            u_low_part(2 * NB - 1)

            def codes(r, k):
                if k % 4 == 0:
                    dve.wait_ge(a8_in[k // 4], (r * 16) + 16)
                dve.wait_ge(g1_ready, r * NK + k - 3) if not (isinstance(r, int) and r == 0 and k < 4) else None
                for u in range(2):
                    t = 2 * k + u
                    a = a8ring[t // 8][:, (t % 8) * BW:(t % 8 + 1) * BW]
                    row = t_row[:, bass.ds(r * BW, BW)] if not isinstance(r, int) else t_row[:, r * BW:(r + 1) * BW]
                    last = dve.scalar_tensor_tensor(code[k % 4][:, u * BW:(u + 1) * BW], row, neg_s[:, t:t + 1], a,
                                                    ALU.is_gt, ALU.add)
                last.then_inc(code_ready, 1)

            def not_positive(r, k, first):
                dve.wait_ge(code_ready, r * NK + (k + 1))
                gate_free(dve, r, k, first)
                dve.tensor_scalar(gate[1][k % 4], code[k % 4], float(ONE8), None, ALU.is_equal).then_inc(g2_ready, 1)

            def gat_result(r, step):
                if step == 0:
                    dve.wait_ge(z_sum, r + 1)
                    for s in range(BT):
                        rcol = rr[:, bass.ds(r * BT + s, 1)] if not isinstance(r, int) else rr[:, r * BT + s:r * BT + s + 1]
                        last = dve.scalar_tensor_tensor(zs[:, 2 * s, 0:UW], zs[:, 2 * s, 0:UW], rcol,
                                                        zs[:, 2 * s + 1, 0:UW], ALU.mult, ALU.add)
                    lap.step(dve, last)
                    even = zs.rearrange("p (s g) c -> p s g c", g=2)[:, :, 0, D]
                    lap.step(dve, dve.tensor_scalar(den4, even, 1.0 / S, None, ALU.mult))
                    lap.step(dve, dve.reciprocal(den4, den4))
                    dve.wait_ge(done, r * 16)
                    for s in range(BT):
                        xt = x3n[:, bass.ds(r * BT + s, 1), :].rearrange("p t d -> p (t d)") if not isinstance(r, int) \
                            else x3n[:, r * BT + s, :]
                        last = dve.scalar_tensor_tensor(outs[:, s, :], zs[:, 2 * s, 0:D], den4[:, s:s + 1], xt,
                                                        ALU.mult, ALU.add)
                    last.then_inc(zz_ready, 1)
                if step == 1:
                    dve.wait_ge(zz_ready, r + 1)
                    moments(outs, 0)
                if step == 2:
                    normed(outs, outs, r + (3 * NB + 1), out_ready)

            def gat_round(r, first):
                for k in range(NK):
                    codes(r, k)
                    if k:
                        not_positive(r, k - 1, first)
                    elif not first:
                        not_positive(r - 1, NK - 1, False)
                    if not first and k in (8, 9, 12):
                        gat_result(r - 1, (8, 9, 12).index(k))

            lap.base, lap.per = lap.base + 1, 4
            gat_round(0, True)
            with dve.Fori(1, NB) as r:
                lap.start(r - 1)
                gat_round(r, False)
            not_positive(NB - 1, NK - 1, False)
            lap.start(NB - 1)
            for step in range(3):
                gat_result(NB - 1, step)

        @block.tensor
        def _(pe):
            zeros = zero16[:, :].rearrange("p (o c) -> p o c", o=1).to_broadcast([P, 4, P])
            pe.wait_ge(const_ready, 1)
            for h in range(2):
                if h:
                    pe.wait_ge(agg_kept, 4)
                for j in range(4):
                    pe.matmul(ps[:, j, :], zero16[:, :], zeros, start=True, stop=False)
                with pe.Fori(0, NB) as g:
                    for s in range(4):
                        pe.wait_ge(row_cast[s], g + (h * NB + 1))
                        pe.wait_ge(xs_copied[s], g + (h * NB + 1))
                        pe.wait_ge(at_written[s % 2], g * 2 + (h * NB * 2 + s // 2))
                        pairs = rows8[s].bitcast(F16)
                        trans = ps[:, 4 + s % 2, :].bitcast(F16)
                        for k in range(HK):
                            last = pe.transpose(trans[:, k * P:(k + 1) * P], pairs[:, k * P:(k + 1) * P],
                                                ident16[:, :])
                        last.then_inc(at_ps[s], 1)
                        cols = rows8[s].rearrange("p (j k q b) -> p j k b q", j=4, k=2, b=2)
                        for part in range(2):
                            for j in range(4):
                                last = pe.matmul(ps[:, j, :], xs_tile[:, s, part, :], cols[:, j],
                                                 start=False, stop=False)
                        last.then_inc(row_used[s], 1)
                for j in range(4):
                    pe.matmul(ps[:, j, :], zero16[:, :], zeros, start=False, stop=True).then_inc(agg_ps, 1)
            pe.wait_ge(xn_in, 16)
            pe.wait_ge(agg_kept, 8)
            for r in range(NB):
                if r >= 2:
                    pe.wait_ge(xt_kept, r - 1)
                for s in range(BT):
                    last = pe.transpose(ps[:, r % 2, s * P:(s + 1) * P], xn[:, r * BT + s, :], ident[:, :])
                last.then_inc(xt_ps, 1)
            pe.wait_ge(rdeg_ready, 1)
            for r in range(NB + 1):
                if r < NB:
                    if r >= 2:
                        pe.wait_ge(agg_scaled, r - 1)
                    for s in range(BT):
                        t = r * BT + s
                        last = pe.matmul(ps[:, 2 + r % 2, s * P:(s + 1) * P], rdeg[:, t:t + 1].to_broadcast([P, P]),
                                         ident[:, :], start=True, stop=True)
                    last.then_inc(rb_ps, 1)
                if r:
                    q = r - 1
                    pe.wait_ge(agg_scaled, q + 1)
                    pe.wait_ge(xt_kept, q + 1)
                    if q >= 2:
                        pe.wait_ge(h_kept, q - 1)
                    pe.matmul(ps[:, 4 + q % 2, :], wn_s, aggT[:, q * BW:(q + 1) * BW], start=True, stop=False)
                    pe.matmul(ps[:, 4 + q % 2, :], wc_s, x1T[:, q * BW:(q + 1) * BW], start=False, stop=True
                              ).then_inc(h_ps, 1)
            for r in range(NB + 1):
                if r < NB:
                    pe.wait_ge(h_relu, r + 1)
                    if r >= 2:
                        pe.wait_ge(z_ready, r - 1)
                    for s in range(BT):
                        last = pe.transpose(ps[:, 6 + r % 2, s * P:(s + 1) * P],
                                            aggT[:, r * BW + s * P:r * BW + (s + 1) * P], ident[:, :])
                    last.then_inc(r_ps, 1)
                if r:
                    q = r - 1
                    pe.wait_ge(xs_ready, q + 1)
                    if q >= 2:
                        pe.wait_ge(x1t_kept, q - 1)
                    for s in range(BT):
                        last = pe.transpose(ps[:, q % 2, s * P:(s + 1) * P], xn[:, q * BT + s, :], ident[:, :])
                    last.then_inc(x1t_ps, 1)

            def strip_product(r, n, c, parts):
                pe.wait_ge(ring_in[c], r * 16 + (n + 1) * 16)
                if c == 0:
                    pe.wait_ge(prod_kept, r + n)
                    pe.matmul(ps[:, 0, :], zero16[:, :], zeros, start=True, stop=False)
                else:
                    pe.matmul(ps[:, 0, 0:64], zero16[:, :], zero16[:, 0:64], start=False, stop=False)
                strip = ring[c].rearrange("p (k i b) -> p k b i", k=4, b=2)
                for k in range(4):
                    for b in range(2):
                        t = 2 * (4 * c + k) + b
                        for part in range(2):
                            last_one = c == 3 and k == 3 and b == 1 and part == 1
                            last = pe.matmul(ps[:, 0, :], parts[:, t, part * D:(part + 1) * D], strip[:, k, b, :],
                                             start=False, stop=last_one and n == 0)
                if c < 3:
                    last.then_inc(strip_used[c], 1)
                elif n == 0:
                    last.then_inc(prod_ps, 1)

            def x1_block(r):
                return x1T[:, r * BW:(r + 1) * BW] if isinstance(r, int) else x1T[:, bass.ds(r * BW, BW)]

            def mix(r):
                pe.wait_ge(prod_kept, r + 1)
                pe.wait_ge(vt_kept, r)
                pe.matmul(ps[:, 1, :], w_1, x1_block(r), start=True, stop=False)
                pe.matmul(ps[:, 1, :], w_2, tmp[0], start=False, stop=True).then_inc(vt_ps, 1)

            def four_transposes(bank, src, signal):
                for s in range(BT):
                    last = pe.transpose(ps[:, bank, s * P:(s + 1) * P], src[:, s * P:(s + 1) * P], ident[:, :])
                last.then_inc(signal, 1)

            def mixed_nodes(r):
                pe.wait_ge(vt_kept, r + 1)
                pe.wait_ge(vn_kept, r)
                four_transposes(2, tmp[1], vn_ps)

            def first_round(r, first):
                strip_product(r, 0, 0, xp)
                if not first:
                    mix(r - 1)
                strip_product(r, 0, 1, xp)
                if not first:
                    mixed_nodes(r - 1)
                strip_product(r, 0, 2, xp)
                strip_product(r, 0, 3, xp)

            pe.wait_ge(x1_low, NB)
            pe.wait_ge(x1t_kept, NB)
            first_round(0, True)
            with pe.Fori(1, NB) as r:
                first_round(r, False)
            mix(NB - 1)
            mixed_nodes(NB - 1)

            def nodes_out(r):
                pe.wait_ge(prod_kept, r + (NB + 1))
                pe.wait_ge(x2s_ready, r)
                four_transposes(1, tmp[0], o_ps)

            def cos_operand(r):
                pe.wait_ge(y_ready, r + 1)
                pe.wait_ge(y_kept, r)
                four_transposes(2, tmp[2], y_ps)

            def second_round(r, first):
                strip_product(r, NB, 0, vp)
                if not first:
                    nodes_out(r - 1)
                for c in (1, 2, 3):
                    strip_product(r, NB, c, vp)
                if not first:
                    cos_operand(r - 1)
                pe.matmul(ps[:, 0, :], w_b, x1_block(r), start=False, stop=True).then_inc(prod_ps, 1)

            pe.wait_ge(vn_kept, NB)
            second_round(0, True)
            with pe.Fori(1, NB) as r:
                second_round(r, False)
            nodes_out(NB - 1)
            cos_operand(NB - 1)

            def cosines(r, k, first):
                if not (first and k < 2):
                    pe.wait_ge(exp_ready[k % 2], r * (NK // 2) + k // 2)
                def block_part(h):
                    return yT[:, bass.ds(r, 1), h, :].rearrange("p r i -> p (r i)") if not isinstance(r, int) \
                        else yT[:, r, h, :]
                for b in range(2):
                    t = 2 * k + b
                    def tile(h):
                        return yT[:, t // BT, h, (t % BT) * P:(t % BT + 1) * P]
                    bank = ps[:, 4 + 2 * (k % 2) + b, :]
                    pe.matmul(bank, tile(0), block_part(0), start=True, stop=False)
                    pe.matmul(bank, tile(0), block_part(1), start=False, stop=False)
                    last = pe.matmul(bank, tile(1), block_part(0), start=False, stop=True)
                last.then_inc(s_ps[k % 2], 1)

            def weighted_sums(r, k, first):
                pe.wait_ge(low_ready[k % 4], r * 4 + (k // 4 + 1))
                for b in range(2):
                    t = 2 * k + b
                    for s in range(BT):
                        at_ = b * BW + s * P
                        if t == 0 and not first:
                            pe.wait_ge(pv_kept, r * BT + (s + 1 - BT))
                        pe.matmul(ps[:, s, 0:PARTS], ehigh[k % 4][:, at_:at_ + P], xp[:, t, :],
                                  start=(t == 0), stop=False)
                        last = pe.matmul(ps[:, s, D:PARTS], elow[k % 4][:, at_:at_ + P], xp[:, t, D:PARTS],
                                         start=False, stop=(t == NT - 1))
                last.then_inc(pv_done[k % 4], 1)

            def attention_round(r, first):
                for k in range(NK):
                    cosines(r, k, first)
                    if k >= LAG:
                        weighted_sums(r, k - LAG, first)
                    elif not first:
                        weighted_sums(r - 1, NK + k - LAG, first)

            pe.wait_ge(y_kept, NB)
            pe.wait_ge(x2_low, NB)
            attention_round(0, True)
            with pe.Fori(1, NB) as r:
                attention_round(r, False)
            for k in range(NK - LAG, NK):
                weighted_sums(NB - 1, k, False)

            pe.wait_ge(w3_in, 48)
            for j in range(2):
                pe.wait_ge(exp_ready[j], NB * NK // 2)
            pe.matmul(ps[:, 4, 0:2], w3s, atts, start=True, stop=True).then_inc(v_ps, 1)
            pe.wait_ge(x3_in, 16)
            pe.wait_ge(pv_kept, BT * NB)
            for r in range(NB):
                if r >= 2:
                    pe.wait_ge(x3t_kept, r - 1)
                four_transposes(r % 2, x3n[:, r * BT:(r + 1) * BT, :].rearrange("p t d -> p (t d)"), x3t_ps)
                pe.wait_ge(x3t_kept, r + 1)
                pe.wait_ge(v_ready, 1)
                if r >= 2:
                    pe.wait_ge(h_out, r - 1)
                    pe.wait_ge(st_out, r - 1)
                    pe.wait_ge(t_out, r - 1)
                for s in range(BT):
                    tile = x3T[:, (r * BT + s) * P:(r * BT + s + 1) * P]
                    pe.matmul(ps[:, 2 + r % 2, s * P:(s + 1) * P], tile, w3Ts, start=True, stop=True)
                    last = pe.matmul(ps[:, 4 + r % 2, 2 * s:2 * s + 2], tile, vst, start=True, stop=True)
                last.then_inc(hst_ps, 1)
                pe.matmul(ps[:, 6 + r % 2, :], vrow, x3T[:, r * BW:(r + 1) * BW], start=True, stop=True
                          ).then_inc(t_ps, 1)
            pe.wait_ge(mx_ready, 1)
            pe.transpose(ps[0:1, 0, 0:P], mx, ident[:, :]).then_inc(mx_ps, 1)
            pe.wait_ge(mx_ready, 2)
            pe.matmul(ps[:, 0, 0:1], ones_row[0:1, :], mxrow[0:1, :], start=True, stop=True).then_inc(mx_ps, 1)

            def gated_sums(r, k, first):
                if k == 0 and first:
                    pe.wait_ge(h_out, NB)
                    pe.wait_ge(st_out, NB)
                    pe.wait_ge(t_out, NB)
                    pe.wait_ge(mall_ready, 1)
                if first:
                    pe.wait_ge(u_low, 2 * (2 * k // BT) + 2)
                pe.wait_ge(g1_ready, r * NK + (k + 1))
                pe.wait_ge(g2_ready, r * NK + (k + 1))
                pairs = [(u, s, g) for u in range(2) for s in range(BT) for g in range(2)]
                if k == NK - 1:
                    pairs = [(u, s, g) for s in range(BT) for g in range(2) for u in range(2)]
                for u, s, g in pairs:
                    t = 2 * k + u
                    nodes = gate[g][k % 4][:, u * BW:(u + 1) * BW].rearrange("p (k q b) -> p k b q", k=2, b=2)
                    if t == 0 and not first:
                        pe.wait_ge(z_kept, r * 8 + (2 * s + g + 1 - 8))
                    last = pe.matmul(ps[:, 2 * s + g, 0:2 * UW], nodes[:, s // 2, s % 2, :], ug[g][:, t, :],
                                     start=(t == 0), stop=(t == NT - 1))
                    if t == NT - 1:
                        last.then_inc(z_ps, 1)
                if k < NK - 1:
                    last.then_inc(gates_used[k % 4], 1)

            for k in range(NK):
                gated_sums(0, k, True)
            with pe.Fori(1, NB) as r:
                for k in range(NK):
                    gated_sums(r, k, False)


def kernel(**inputs):
    import numpy as _np
    import concourse.bacc as _bacc
    from concourse import mybir as _mybir
    from concourse.bass_utils import run_bass_kernel_spmd as _run

    nc = _bacc.Bacc("TRN2", target_bir_lowering=False, num_devices=1)
    a = {k: _np.asarray(v) for k, v in inputs.items()}
    laid = [("x", a["x"]), ("adj", a["adj"]), ("wnT", a["L0_gnn_W_n"].T), ("wcT", a["L0_gnn_W_c"].T),
            ("bn", a["L0_gnn_b_n"]), ("bc", a["L0_gnn_b_c"]), ("gamma", a["L0_gnn_gamma"]),
            ("beta", a["L0_gnn_beta"]), ("w1", a["L1_gnn_weight"]), ("b1", a["L1_gnn_bias"]),
            ("cos_beta", a["L2_gnn_beta"]), ("w3", a["L3_gnn_weight"]), ("w3T", a["L3_gnn_weight"].T),
            ("att", _np.stack([a["L3_gnn_att_src"][0], a["L3_gnn_att_dst"][0]], axis=1))]
    arrays, args = {}, []
    for name, v in laid:
        arrays[f"in_{name}"] = _np.ascontiguousarray(v)
        args.append(nc.dram_tensor(f"in_{name}", v.shape, _mybir.dt.from_np(v.dtype), kind="ExternalInput").ap())
    args.append(nc.dram_tensor("out_0", (4096, 128), _mybir.dt.float32, kind="ExternalOutput").ap())
    program(nc, *args)
    r = _run(nc, [arrays], core_ids=[0])
    return r.results[0]["out_0"]
```

```python
from contextlib import ExitStack

import concourse.bass as bass
from concourse import mybir

F32 = mybir.dt.float32
F16 = mybir.dt.float16
F8 = mybir.dt.float8e5
U16 = mybir.dt.uint16
U8 = mybir.dt.uint8
ALU = mybir.AluOpType
ACT = mybir.ActivationFunctionType
AX_X = mybir.AxisListType.X

P = 128
N = 4096
D = 128
NT = N // P
BT = 4
NB = NT // BT
BW = BT * P
NK = NT // 2
HK = NK // 2
LN_EPS = 1e-5
COS_EPS = 1e-7
ONE8 = 60
X0_SCALE = 16.0
S = 4096.0
HS = 256.0
PARTS = 2 * D + 1
UW = D + 1
KB = 1024
SMALL = 328


class Lap:

    def __init__(self, sem, per=0, base=0):
        self.sem, self.per, self.base, self.round, self.n = sem, per, base, 0, 0

    def start(self, r):
        self.round, self.n = r, 0

    def done(self, ins):
        ins.then_inc(self.sem, 1)
        self.n += 1

    def wait(self, eng):
        eng.wait_ge(self.sem, self.round * self.per + (self.base + self.n))

    def step(self, eng, ins):
        self.done(ins)
        self.wait(eng)


def program(nc, x, adj, wnT, wcT, bn, bc, gamma, beta, w1, b1, cos_beta, w3, w3T, att, out):
    adj_rows = adj.rearrange("(r k p b) c -> r k b p c", r=NB, k=2, b=2)
    adj_casts = adj.rearrange("(k p b) (i c) -> i b p k c", p=P, b=2, c=BW)
    x_nodes = x.rearrange("(k p b) d -> p k (b d)", p=P, b=2)
    out_nodes = out.rearrange("(r k p b) d -> r p k (b d)", r=NB, k=2, b=2)
    a8_dram = nc.dram_tensor("a8_dram", (P, NB * NT, BW), F8).ap()
    a8_blocks = a8_dram.rearrange("p (i k b) c -> i b p k c", i=NB, b=2)
    a8_strips = a8_dram.rearrange("p (s t) c -> s p (t c)", t=8)

    with ExitStack() as ctx:
        def sb(name, shape, dt):
            return ctx.enter_context(nc.sbuf_tensor(name, shape, dt))

        def sem(name):
            return ctx.enter_context(nc.semaphore(name))

        def sems(name, n):
            return [sem(f"{name}{i}") for i in range(n)]

        at = sb("at", [P, NB * NK * BW * 2], U8)
        work = sb("work", [P, 73984], U8)
        ident = sb("ident", [P, P], F32)
        ident16 = sb("ident16", [P, P], F16)
        weights = sb("weights", [P, 5, D], F32)
        small = sb("small", [P, SMALL], F32)

        ps = ctx.enter_context(nc.psum_tensor("ps", [P, 8, 512], F32))

        def view(a, n, dt):
            return work[:, a:a + n].bitcast(dt)

        LD0, NAT0, XP0, AGG0 = 0, 32 * KB, 40 * KB, 40 * KB + NT * PARTS * 2 + 64
        rows = [view(LD0 + 8 * KB * s, 8 * KB, F32) for s in range(4)]
        rows8 = [view(NAT0 + 2 * KB * s, 2 * KB, F8) for s in range(4)]
        xp = view(XP0, NT * PARTS * 2, F16).rearrange("p (t c) -> p t c", t=NT)
        aggT = view(AGG0, 16 * KB, F32)
        xn = view(0, 16 * KB, F32).rearrange("p (t d) -> p t d", t=NT)
        x1T = view(16 * KB, 16 * KB, F32)
        ring = [view(4 * KB * c, 4 * KB, F8) for c in range(4)]
        vp = view(AGG0, 16 * KB, F16).rearrange("p (t c) -> p t c", t=NT)
        tmp = [view(NAT0 + 2 * KB * s, 2 * KB, F32) for s in range(4)]
        yT = view(16 * KB, 16 * KB, F16).rearrange("p (r h i) -> p r h i", r=NB, h=2)
        small_n = [0]

        def col(n=1):
            a = small_n[0]
            small_n[0] += n
            return small[:, a:a + n]

        bnc, bcc, hbias, gam, bet, b1c, cosb, cscale, cbias = [col() for _ in range(9)]
        deg4 = col(4)
        degp = col(2 * NT)
        rdeg = col(NT)
        eq0 = col(NT)
        bstat = col(NB * 6)
        bagg, bscale, btmp = col(2), col(), col()
        stat4 = col(BT * 6).rearrange("p (t c) -> p t c", t=BT)
        mv4 = col(BT * 2).rearrange("p (t c) -> p t c", t=BT)
        va4, rs4, half4, n24, rn4, va4b, s4, eps4, epss4, epsc4 = [col(BT) for _ in range(10)]
        stat4b = col(BT * 6).rearrange("p (t c) -> p t c", t=BT)
        mv4b = col(BT * 2).rearrange("p (t c) -> p t c", t=BT)
        rs4b, bshift = col(BT), col()
        minus4, nmean4, minus60, carry = col(BT), col(BT), col(), col()
        assert small_n[0] <= SMALL
        w_1, w_2, w_b, wn_s, wc_s = [weights[:, j, :] for j in range(5)]

        LAG = 3
        expo = [view(4 * KB * j, 4 * KB, F32) for j in range(4)]
        ehigh = [view(AGG0 + 4 * KB * j, 2 * KB, F16) for j in range(4)]
        elow = [view(AGG0 + 4 * KB * j + 2 * KB, 2 * KB, F16) for j in range(4)]
        psum_kept = view(NAT0, BT * PARTS * 4, F32).rearrange("p (s c) -> p s c", s=BT)
        res4 = view(NAT0 + BT * PARTS * 4 + 16, BT * D * 4, F32).rearrange("p (s d) -> p s d", s=BT)
        place = [0]

        def late(n, dt, size):
            a = place[0]
            place[0] += (n * size + 31) // 32 * 32
            return at[:, a:a + n * size].bitcast(dt)

        x3n = late(NT * D, F32, 4).rearrange("p (t d) -> p t d", t=NT)
        w3s, w3Ts, vrow = late(D, F32, 4), late(D, F32, 4), late(D, F32, 4)
        atts, vst = late(2, F32, 4), late(2, F32, 4)
        assert place[0] <= 32 * KB
        x3T = late(N, F32, 4)
        t_row = late(N, F32, 4)
        hx = late(NT * UW, F32, 4).rearrange("p (t c) -> p t c", t=NT)
        ug = [late(NT * 2 * UW, F16, 2).rearrange("p (t c) -> p t c", t=NT) for _ in range(2)]
        uf = [late(BT * UW, F32, 4).rearrange("p (t c) -> p t c", t=BT) for _ in range(2)]
        zs = late(8 * 2 * UW, F32, 4).rearrange("p (j c) -> p j c", j=8)
        zz = late(BT * UW, F32, 4).rearrange("p (s c) -> p s c", s=BT)
        st = late(2 * NT, F32, 4).rearrange("p (t c) -> p t c", t=NT)
        neg_s, wt1, wt2, rr = late(NT, F32, 4), late(NT, F32, 4), late(NT, F32, 4), late(NT, F32, 4)
        mx, mxrow, mall, ones_row = late(1, F32, 4), late(1, F32, 4), late(4, F32, 4), late(P, F32, 4)
        den4 = late(BT, F32, 4)
        assert place[0] <= 128 * KB
        a8ring = [view(4 * KB * c, 4 * KB, U8) for c in range(4)]
        code = [view(16 * KB + 2 * KB * j, 2 * KB, F16) for j in range(4)]
        gate = [[view((24 + 8 * g) * KB + 2 * KB * j, 2 * KB, F16) for j in range(4)] for g in range(2)]
        outs = view(40 * KB, BT * D * 4, F32).rearrange("p (s d) -> p s d", s=BT)

        const_in, const_ready = sem("const_in"), sem("const_ready")
        x_in, row_in = sems("x_in", 4), sems("row_in", 4)
        x_high, x_low = sem("x_high"), sem("x_low")
        row_cast, deg_kept, xs_copied = sems("row_cast", 4), sems("deg_kept", 4), sems("xs_copied", 4)
        row_used, at_ps, at_written = sems("row_used", 4), sems("at_ps", 4), sems("at_written", 2)
        agg_ps, agg_kept = sem("agg_ps"), sem("agg_kept")
        dve_lap, pool_lap, act_lap = sem("dve_lap"), sem("pool_lap"), sem("act_lap")
        xn_in, xt_ps, xt_kept = sem("xn_in"), sem("xt_ps"), sem("xt_kept")
        rdeg_ready, rb_ps, agg_scaled = sem("rdeg_ready"), sem("rb_ps"), sem("agg_scaled")
        h_ps, h_kept, h_norm, h_relu = sem("h_ps"), sem("h_kept"), sem("h_norm"), sem("h_relu")
        bvar_ready, brstd_ready = sem("bvar_ready"), sem("brstd_ready")
        r_ps, z_ready, var_ready, rstd_ready = sem("r_ps"), sem("z_ready"), sem("var_ready"), sem("rstd_ready")
        xs_ready, x1_high, x1_low, x1t_ps, x1t_kept = (sem("xs_ready"), sem("x1_high"), sem("x1_low"),
                                                       sem("x1t_ps"), sem("x1t_kept"))
        ring_in, strip_used = sems("ring_in", 4), sems("strip_used", 3)
        prod_ps, prod_kept = sem("prod_ps"), sem("prod_kept")
        ring_done = strip_used + [prod_ps]
        x1_here, vn_ps, vn_kept = sem("x1_here"), sem("vn_ps"), sem("vn_kept")
        o_ps, x2s_ready, x2_high, x2_low = sem("o_ps"), sem("x2s_ready"), sem("x2_high"), sem("x2_low")
        sq_ready, rn_ready, y_ready, y_ps = sem("sq_ready"), sem("rn_ready"), sem("y_ready"), sem("y_ps")
        y_high, y_kept, a8_out = sem("y_high"), sem("y_kept"), sems("a8_out", 2)
        s_ps, exp_ready, mask_ready = sems("s_ps", 2), sems("exp_ready", 2), sem("mask_ready")
        high_ready, low_ready, pv_done = sem("high_ready"), sems("low_ready", 4), sems("pv_done", 4)
        pv_kept, num_ready, res_ready, res_norm = (sem("pv_kept"), sem("num_ready"), sem("res_ready"),
                                                           sem("res_norm"))
        w3_in, v_lap, h3_ps, st_ps, g2_fourth = sem("w3_in"), sem("v_lap"), sem("h3_ps"), sem("st_ps"), sem("g2_fourth")
        v_ps, v_ready, x3t_ps, x3t_kept, t_ps = (sem("v_ps"), sem("v_ready"), sem("x3t_ps"), sem("x3t_kept"),
                                                 sem("t_ps"))
        h_out, st_out, t_out, mx_ps, mall_ready, w_ready = (sem("h_out"), sem("st_out"), sem("t_out"), sem("mx_ps"),
                                                            sem("mall_ready"), sem("w_ready"))
        uf_ready, u_high, u_low = sem("uf_ready"), sem("u_high"), sem("u_low")
        a8_in, code_ready, g1_ready, g2_ready = sems("a8_in", 4), sem("code_ready"), sem("g1_ready"), sem("g2_ready")
        gates_used, z_ps, z_kept, z_sum = sems("gates_used", 4), sem("z_ps"), sem("z_kept"), sem("z_sum")
        zz_ready, out_ready, mx_ready = sem("zz_ready"), sem("out_ready"), sem("mx_ready")
        xs_tile = sb("xs_tile", [P, 4, 2, D], F16)
        zero16 = sb("zero16", [P, P], F16)
        stored = sem("stored")

        block = ctx.enter_context(nc.Block())

        def node_block(v, r):
            return v[:, r * BT:(r + 1) * BT, :]

        R_BANKS = (6, 7, 3, 2)

        X3_BANKS, H_BANK, T_BANKS = (4, 6), 7, (5, 4, 6)
        EARLY_H = 5
        LATER = [("t", 0), ("h", 5), ("t", 1), ("h", 6), ("t", 2), ("h", 7)] + [("t", r) for r in range(3, NB)]

        def row_col(v, r, s):
            return v[:, r * BT + s:r * BT + s + 1] if isinstance(r, int) else v[:, bass.ds(r * BT + s, 1)]

        def gate_free(eng, r, k, first):
            if k % 4 < 3:
                eng.wait_ge(gates_used[k % 4], r * 4 + k // 4)
            elif k > 3:
                eng.wait_ge(gates_used[3], r * 3 + k // 4)
            elif not first:
                eng.wait_ge(z_ps, r * 8)

        @block.sync
        def _(sp):
            xk = aggT.rearrange("p (k c) -> p k c", k=NK)

            def load_rows(g, h, first):
                for s in range(4):
                    if first:
                        sp.dma_start(xk[:, 4 * s:4 * s + 4, :], x_nodes[:, 4 * s:4 * s + 4, :]).then_inc(x_in[s], 16)
                    else:
                        sp.wait_ge(row_cast[s], g + h * NB)
                    sp.dma_start(rows[s], adj_rows[bass.ds(g, 1), s // 2, s % 2, :, h * 2048:(h + 1) * 2048]
                                 .rearrange("r p c -> (r p) c")).then_inc(row_in[s], 16)

            load_rows(0, 0, True)
            for h in range(2):
                with sp.Fori(1 - h, NB) as g:
                    load_rows(g, h, False)
            for s in range(2):
                sp.wait_ge(row_cast[s], 2 * NB)
            sp.dma_start(xn.rearrange("p (k b) d -> p k (b d)", b=2), x_nodes).then_inc(xn_in, 16)
            for n in range(2):
                if n == 0:
                    for c in range(4):
                        for q in (x1_low, x1_high, x1t_ps):
                            sp.wait_ge(q, 2 * c + 2)
                        sp.dma_start(ring[c].bitcast(U8), at[:, c * 4 * KB:(c + 1) * 4 * KB]
                                     ).then_inc(ring_in[c], 16)
                with sp.Fori(1 - n, NB) as r:
                    for c in range(4):
                        sp.wait_ge(ring_done[c], r + n * NB)
                        sp.dma_start(ring[c].bitcast(U8), at[:, bass.ds((r * 4 + c) * (4 * KB), 4 * KB)]
                                     ).then_inc(ring_in[c], 16)
            sp.wait_ge(mask_ready, (NB - 1) * NK)
            sp.dma_start(w3s, w3).then_inc(w3_in, 16)
            sp.dma_start(w3Ts, w3T).then_inc(w3_in, 16)
            sp.dma_start(atts, att).then_inc(w3_in, 16)
            for q in a8_out:
                sp.wait_ge(q, 16 * NB)
            for j in range(4):
                sp.wait_ge(low_ready[j], NB * 4)
            for r in range(NB + 2):
                for c in range(4 if r < NB else 0):
                    if r:
                        sp.wait_ge(code_ready, r * NK + (4 * c + 4 - NK))
                    sp.dma_start(a8ring[c], a8_strips[r * 4 + c].bitcast(U8)).then_inc(a8_in[c], 16)
                if r >= 2:
                    sp.wait_ge(out_ready, r - 1)
                    sp.dma_start(out_nodes[r - 2], outs.rearrange("p (k b) d -> p k (b d)", k=2)
                                 ).then_inc(stored, 16)
            sp.wait_ge(stored, 16 * NB + 1)

        @block.gpsimd
        def _(pool):
            lap = Lap(pool_lap)
            lap.step(pool, pool.memset(ident[:, :], 0.0))
            lap.step(pool, pool.affine_select(out=ident[:, :], in_=ident[:, :], compare_op=ALU.not_equal, fill=1.0,
                                              base=0, pattern=[[-1, P]], channel_multiplier=1))
            pool.tensor_copy(ident16[:, :], ident[:, :])
            pool.memset(zero16[:, :], 0.0)
            for dst, value in ((s4, S), (eps4, LN_EPS), (epss4, LN_EPS * S * S), (epsc4, COS_EPS)):
                pool.memset(dst, value)
            pool.memset(minus4, -1.0)
            pool.memset(minus60, -float(ONE8))
            pool.memset(half4, -0.5).then_inc(const_ready, 1)

            def inverse_root(dst, value, eps, signal, scale=None):
                lap.step(pool, pool.tensor_tensor(va4, value, eps, ALU.add))
                if scale is None:
                    pool.tensor_tensor(dst, va4, half4, ALU.pow).then_inc(signal, 1)
                else:
                    lap.step(pool, pool.tensor_tensor(dst, va4, half4, ALU.pow))
                    pool.tensor_tensor(dst, dst, scale, ALU.mult).then_inc(signal, 1)

            for dst, src in ((wn_s, wnT), (wc_s, wcT), (w_1, w1[1]), (w_2, w1[2]), (w_b, w1[0])):
                pool.dma_start(dst, src).then_inc(const_in, 16)
            for dst, src in ((bnc, bn), (bcc, bc), (gam, gamma), (bet, beta), (b1c, b1)):
                pool.dma_start(dst, src.rearrange("(p o) -> p o", o=1)).then_inc(const_in, 16)
            pool.dma_start(cosb, cos_beta.rearrange("(p o) -> p o", o=1).to_broadcast([P, 1])
                           ).then_inc(const_in, 16)
            pool.wait_ge(x_low, 1)
            pool.wait_ge(x_high, 1)
            def stationary_copies(g, h, first):
                for s in range(4):
                    if not first:
                        pool.wait_ge(row_used[s], g + h * NB)
                    pool.tensor_copy(xs_tile[:, s, :, :].rearrange("p h d -> p (h d)"),
                                     xp[:, bass.ds(g * BT + s, 1), 0:2 * D].rearrange("p t c -> p (t c)")
                                     ).then_inc(xs_copied[s], 1)
                    pool.wait_ge(row_cast[s], g + (h * NB + 1))
                    pool.tensor_copy(degp[:, bass.ds(g * BT + (h * NT + s), 1)], deg4[:, s:s + 1]
                                     ).then_inc(deg_kept[s], 1)

            stationary_copies(0, 0, True)
            pool.wait_ge(x_low, 4)
            pool.wait_ge(x_high, 4)
            for h in range(2):
                with pool.Fori(1 - h, NB) as g:
                    stationary_copies(g, h, False)
            pool.wait_ge(bvar_ready, 1)
            lap.step(pool, pool.tensor_scalar(bscale, bagg[:, 1:2], LN_EPS, None, ALU.add))
            lap.step(pool, pool.tensor_tensor(bscale, bscale, half4[:, 0:1], ALU.pow))
            lap.step(pool, pool.tensor_tensor(bscale, bscale, gam, ALU.mult))
            lap.step(pool, pool.tensor_tensor(bshift, bagg[:, 0:1], bscale, ALU.mult))
            pool.tensor_tensor(bshift, bet, bshift, ALU.subtract).then_inc(brstd_ready, 1)

            def low(r):
                pool.wait_ge(x1_high, r + 1)
                pool.tensor_tensor(node_block(xp, r)[:, :, 0:D], node_block(xn, r), node_block(xp, r)[:, :, D:2 * D],
                                   ALU.subtract).then_inc(x1_low, 1)

            for r in range(NB):
                pool.wait_ge(var_ready, r + 1)
                inverse_root((rs4, rs4b)[r % 2], (mv4, mv4b)[r % 2][:, :, 1], eps4, rstd_ready, s4)
                if r:
                    low(r - 1)
            low(NB - 1)

            pool.wait_ge(x1t_kept, NB)
            pool.tensor_copy(tmp[1], x1T[:, 0:BW]).then_inc(x1_here, 1)
            with pool.Fori(1, NB) as r:
                pool.wait_ge(vn_kept, r)
                pool.tensor_copy(tmp[1], x1T[:, bass.ds(r * BW, BW)]).then_inc(x1_here, 1)

            for r in range(NB):
                pool.wait_ge(var_ready, NB + r + 1)
                inverse_root(rs4, mv4[:, :, 1], eps4, rstd_ready, s4)
                pool.wait_ge(sq_ready, r + 1)
                inverse_root(rn4, n24, epsc4, rn_ready)

            for r in range(NB):
                for b in range(2):
                    if r:
                        pool.wait_ge(a8_out[b], r * 16)
                    pool.dma_start(a8_blocks[r, b], adj_casts[r, b]).then_inc(a8_out[b], 16)
                pool.wait_ge(pv_kept, r * BT + BT)
                if r:
                    pool.wait_ge(res_norm, r)
                lap.step(pool, pool.tensor_tensor(psum_kept[:, :, D:2 * D], psum_kept[:, :, 0:D],
                                                  psum_kept[:, :, D:2 * D], ALU.add))
                pool.tensor_tensor(res4, node_block(xp, r)[:, :, 0:D], node_block(xp, r)[:, :, D:2 * D], ALU.add
                                   ).then_inc(num_ready, 1)
                pool.wait_ge(var_ready, r + (2 * NB + 1))
                inverse_root(rs4, mv4[:, :, 1], epss4, rstd_ready, s4)
            lap.per, lap.base, lap.n = 3, lap.n, 0

            pool.wait_ge(w_ready, 1)

            def weigh(n):
                r, g = n // 2, n % 2
                w = (wt1, wt2)[g][:, r * BT:(r + 1) * BT].rearrange("p (t o) -> p t o", o=1).to_broadcast([P, BT, UW])
                pool.wait_ge(h_out, r + 1)
                if n >= 2:
                    pool.wait_ge(u_low, n - 1)
                pool.tensor_tensor(uf[g], node_block(hx, r), w, ALU.mult).then_inc(uf_ready, 1)

            def fourth_gate(r, k):
                pool.wait_ge(code_ready, r * NK + (k + 1))
                gate_free(pool, r, k, isinstance(r, int) and r == 0)
                pool.tensor_tensor(carry, minus60, minus60, ALU.add)
                pool.tensor_scalar(gate[1][3], code[3], float(ONE8), None, ALU.is_equal).then_inc(g2_fourth, 1)

            def block_sums(r):
                pool.wait_ge(z_kept, r * 8 + 8)
                lap.step(pool, pool.tensor_tensor(zs[:, :, 0:UW], zs[:, :, 0:UW], zs[:, :, UW:2 * UW], ALU.add))
                pool.tensor_tensor(zz, zs[:, 0:BT, 0:UW], zs[:, BT:2 * BT, 0:UW], ALU.add).then_inc(z_sum, 1)

            def block_norm(r):
                pool.wait_ge(var_ready, r + (3 * NB + 1))
                pool.tensor_tensor(nmean4, mv4[:, :, 0], minus4, ALU.mult)
                lap.step(pool, pool.tensor_tensor(va4, mv4[:, :, 1], epss4, ALU.add))
                lap.step(pool, pool.tensor_tensor(rs4, va4, half4, ALU.pow))
                pool.tensor_tensor(nmean4, nmean4, rs4, ALU.mult).then_inc(rstd_ready, 1)

            for k in range(NK):
                weigh(k)
                if k % 4 == 3:
                    fourth_gate(0, k)
            with pool.Fori(1, NB) as r:
                lap.start(r - 1)
                fourth_gate(r, 3)
                block_sums(r - 1)
                fourth_gate(r, 7)
                block_norm(r - 1)
                fourth_gate(r, 11)
                fourth_gate(r, 15)
            lap.start(NB - 1)
            block_sums(NB - 1)
            block_norm(NB - 1)

        @block.scalar
        def _(act):
            xf = aggT.rearrange("p (t d) -> p t d", t=NT)

            def x_high_part(c):
                act.wait_ge(x_in[c], 16)
                act.activation(xp[:, c * 8:(c + 1) * 8, D:2 * D], xf[:, c * 8:(c + 1) * 8, :], ACT.Copy,
                               scale=X0_SCALE).then_inc(x_high, 1)

            def cast_rows(g, h, first):
                for s in range(4):
                    if first:
                        x_high_part(s)
                    act.wait_ge(row_in[s], g * 16 + (h * NB + 1) * 16)
                    if not first:
                        act.wait_ge(row_used[s], g + h * NB)
                        act.wait_ge(deg_kept[s], g + h * NB)
                    act.activation(rows8[s].bitcast(U8), rows[s], ACT.Copy, scale=float(ONE8),
                                   accum_out=deg4[:, s:s + 1]).then_inc(row_cast[s], 1)

            cast_rows(0, 0, True)
            for h in range(2):
                with act.Fori(1 - h, NB) as g:
                    cast_rows(g, h, False)
            for j in (1, 3):
                act.wait_ge(agg_ps, 4 + j + 1)
                act.copy(aggT[:, 2048 + j * BW:2048 + (j + 1) * BW], ps[:, j, :]).then_inc(agg_kept, 1)
            for r in range(NB + 1):
                if r < NB:
                    act.wait_ge(xt_ps, r + 1)
                    act.copy(x1T[:, r * BW:(r + 1) * BW], ps[:, r % 2, :]).then_inc(xt_kept, 1)
                if r:
                    act.wait_ge(h_ps, r)
                    act.activation(aggT[:, (r - 1) * BW:r * BW], ps[:, 4 + (r - 1) % 2, :], ACT.Identity, bias=hbias
                                   ).then_inc(h_kept, 1)

            act.wait_ge(brstd_ready, 1)
            act.wait_ge(h_kept, NB)
            for r in range(NB + 4):
                if r < NB:
                    hb = aggT[:, r * BW:(r + 1) * BW]
                    act.activation(hb, hb, ACT.Relu, bias=bshift, scale=bscale).then_inc(h_relu, 1)
                if 3 <= r < NB + 3:
                    q = r - 3
                    act.wait_ge(xs_ready, q + 1)
                    act.copy(node_block(xp, q)[:, :, D:2 * D], node_block(xn, q)).then_inc(x1_high, 1)
                if r >= 4:
                    q = r - 4
                    act.wait_ge(x1t_ps, q + 1)
                    act.copy(x1T[:, q * BW:(q + 1) * BW], ps[:, 4 + q % 2, :]).then_inc(x1t_kept, 1)

            def first_product(r, first):
                act.wait_ge(prod_ps, r + 1)
                if not first:
                    act.wait_ge(vn_ps, r)
                act.mul(tmp[0], ps[:, 0, :], 1.0 / S).then_inc(prod_kept, 1)

            first_product(0, True)
            with act.Fori(1, NB) as r:
                first_product(r, False)

            def exponentials(r, k, first):
                act.wait_ge(s_ps[k % 2], r * (NK // 2) + (k // 2 + 1))
                if not (first and k < 4):
                    act.wait_ge(low_ready[k % 4], r * 4 + k // 4)
                act.activation(expo[k % 4], ps[:, 4 + 2 * (k % 2):6 + 2 * (k % 2), :].rearrange("p b i -> p (b i)"),
                               ACT.Exp, bias=cbias, scale=cscale).then_inc(exp_ready[k % 2], 1)

            def second_product(r, first):
                act.wait_ge(prod_ps, r + (NB + 1))
                if not first:
                    act.wait_ge(x2s_ready, r)
                act.activation(tmp[0], ps[:, 0, :], ACT.Identity, bias=b1c).then_inc(prod_kept, 1)
                if not first:
                    cos_high(r - 1)
                if isinstance(r, int) and r == NB - 1:
                    exponentials(0, 0, True)
                    exponentials(0, 1, True)
                act.wait_ge(x2s_ready, r + 1)
                x2s = tmp[1].rearrange("p (t d) -> p t d", t=BT)
                act.copy(xp[:, bass.ds(r * BT, BT), D:2 * D], x2s).then_inc(x2_high, 1)
                for s in range(BT):
                    last = act.activation(tmp[3][:, s * D:(s + 1) * D], x2s[:, s, :], ACT.Square, scale=1.0 / S,
                                          accum_out=n24[:, s:s + 1])
                last.then_inc(sq_ready, 1)

            def cos_high(r):
                act.wait_ge(y_ps, r + 1)
                act.copy(yT[:, bass.ds(r, 1), 0, :].rearrange("p r i -> p (r i)"), ps[:, 2, :]).then_inc(y_high, 1)

            second_product(0, True)
            with act.Fori(1, NB - 1) as r:
                second_product(r, False)
            second_product(NB - 1, False)
            cos_high(NB - 1)

            def exp_high(r, k):
                act.wait_ge(mask_ready, r * NK + (k + 1))
                act.wait_ge(pv_done[k % 4], r * 4 + k // 4)
                act.copy(ehigh[k % 4], expo[k % 4]).then_inc(high_ready, 1)

            def keep_sums(r):
                act.wait_ge(pv_done[(NK - 1) % 4], r * 4 + 4)
                for s in range(BT):
                    act.copy(psum_kept[:, s, :], ps[:, s, 0:PARTS]).then_inc(pv_kept, 1)

            def attention_round(r, first):
                for k in range(NK):
                    if k == LAG and not first:
                        keep_sums(r - 1)
                    if not (first and k < 2):
                        exponentials(r, k, first)
                    if k:
                        exp_high(r, k - 1)
                    elif not first:
                        exp_high(r - 1, NK - 1)

            attention_round(0, True)
            with act.Fori(1, NB) as r:
                attention_round(r, False)
            exp_high(NB - 1, NK - 1)
            keep_sums(NB - 1)

            def keep_h(r):
                act.wait_ge(h3_ps, r + 1)
                act.copy(node_block(hx, r)[:, :, 0:D], ps[:, H_BANK, :].rearrange("p (t d) -> p t d", t=BT)
                         ).then_inc(h_out, 1)

            for r in range(NB + 1):
                if r < NB:
                    act.wait_ge(x3t_ps, r + 1)
                    act.copy(x3T[:, r * BW:(r + 1) * BW], ps[:, X3_BANKS[r % 2], :]).then_inc(x3t_kept, 1)
                if 1 <= r <= EARLY_H:
                    keep_h(r - 1)
            act.wait_ge(st_ps, 1)
            act.copy(st.rearrange("p t c -> p (t c)"), ps[:, 5, 0:2 * NT]).then_inc(st_out, 1)

            def u_high_parts(r):
                for g in range(2):
                    act.wait_ge(uf_ready, 2 * r + g + 1)
                    act.copy(node_block(ug[g], r)[:, :, UW:2 * UW], uf[g]).then_inc(u_high, 1)

            def positive(r, k, first):
                act.wait_ge(code_ready, r * NK + (k + 1))
                gate_free(act, r, k, first)
                act.activation(gate[0][k % 4], code[k % 4], ACT.Relu, bias=minus60).then_inc(g1_ready, 1)

            for what, r in LATER:
                if what == "h":
                    keep_h(r)
                else:
                    act.wait_ge(t_ps, r + 1)
                    act.copy(t_row[:, r * BW:(r + 1) * BW].rearrange("p (k q b) -> p k b q", k=2, b=2),
                             ps[:, T_BANKS[r % 3], :].rearrange("p (k b q) -> p k b q", k=2, b=2)
                             ).then_inc(t_out, 1)
                if (what, r) == ("h", EARLY_H + 1):
                    act.wait_ge(mall_ready, 1)
                    act.activation(wt1, st[:, :, 0], ACT.Exp, bias=mall[:, 0:1])
                    act.activation(wt2, st[:, :, 0], ACT.Exp, bias=mall[:, 1:2], scale=0.2).then_inc(w_ready, 1)
                    act.activation(rr, st[:, :, 1], ACT.Exp, bias=mall[:, 2:3], scale=0.8).then_inc(w_ready, 1)
                if (what, r) in (("t", 3), ("t", 5)):
                    u_high_parts((r - 3) // 2)
                if (what, r) in (("t", 4), ("t", 6)):
                    positive(0, (r - 4) // 2, True)

            def keep_z(r):
                for j in range(8):
                    s, g = j // 2, j % 2
                    act.wait_ge(z_ps, r * 8 + (j + 1))
                    if g:
                        last = act.copy(zs[:, BT + s, :], ps[:, j, 0:2 * UW])
                    else:
                        last = act.mul(zs[:, s, :], ps[:, j, 0:2 * UW], row_col(rr, r, s))
                    last.then_inc(z_kept, 1)

            def block_out(r):
                act.wait_ge(rstd_ready, r + (3 * NB + 1))
                for s in range(BT):
                    last = act.activation(outs[:, s, :], outs[:, s, :], ACT.Identity, bias=nmean4[:, s:s + 1],
                                          scale=rs4[:, s:s + 1])
                last.then_inc(out_ready, 1)

            def gat_round(r, first):
                for k in range(NK):
                    if first and k >= 4 and k % 2 == 0:
                        u_high_parts(k // 2)
                    if k == 3 and not first:
                        keep_z(r - 1)
                    if k == 13 and not first:
                        block_out(r - 1)
                    if not (first and k < 2):
                        positive(r, k, first)

            gat_round(0, True)
            with act.Fori(1, NB) as r:
                gat_round(r, False)
            keep_z(NB - 1)
            act.wait_ge(out_ready, NB - 1)
            block_out(NB - 1)

        @block.vector
        def _(dve):
            lap = Lap(dve_lap)
            dve.wait_ge(const_ready, 1)
            xf = aggT.rearrange("p (t d) -> p t d", t=NT)
            def x_low_part(c):
                dve.wait_ge(x_high, c + 1)
                dve.scalar_tensor_tensor(xp[:, c * 8:(c + 1) * 8, 0:D], xf[:, c * 8:(c + 1) * 8, :], X0_SCALE,
                                         xp[:, c * 8:(c + 1) * 8, D:2 * D], ALU.mult, ALU.subtract
                                         ).then_inc(x_low, 1)

            at16 = at[:, :].bitcast(U16)

            def keep_transposed(g, h, first):
                for s in range(4):
                    if first and s < 3:
                        x_low_part(s + 1)
                    dve.wait_ge(at_ps[s], g + (h * NB + 1))
                    src = ps[:, 4 + s % 2, :].bitcast(U16).rearrange("p (k i) -> p k i", k=HK)
                    dst = at16[:, bass.ds(g * (NK * BW) + h * HK * BW, HK * BW)].rearrange(
                        "p (k i) -> p k i", k=HK)[:, :, s * P:(s + 1) * P]
                    dve.tensor_copy(dst, src).then_inc(at_written[s % 2], 1)

            x_low_part(0)
            keep_transposed(0, 0, True)
            dve.wait_ge(const_in, 16 * 11)
            lap.step(dve, dve.tensor_tensor(w_b, w_b, w_2, ALU.subtract))
            lap.step(dve, dve.tensor_tensor(w_b, w_b, ident[:, :], ALU.add))
            dve.tensor_scalar(w_b, w_b, 1.0 / S, None, ALU.mult)
            dve.tensor_scalar(w_1, w_1, 1.0 / S, None, ALU.mult)
            dve.tensor_scalar(w_2, w_2, 2.0, None, ALU.mult)
            dve.tensor_tensor(hbias, bnc, bcc, ALU.add)
            dve.tensor_scalar(cscale, cosb, S ** -2, None, ALU.mult)
            lap.step(dve, dve.tensor_scalar(cbias, cosb, -1.0, None, ALU.mult))
            dve.tensor_tensor(cbias, cosb, cbias, ALU.min).then_inc(const_ready, 1)
            with dve.Fori(1, NB) as g:
                keep_transposed(g, 0, False)
            for j in range(4):
                dve.wait_ge(agg_ps, j + 1)
                dve.tensor_copy(aggT[:, j * BW:(j + 1) * BW], ps[:, j, :]).then_inc(agg_kept, 1)
            with dve.Fori(0, NB) as g:
                keep_transposed(g, 1, False)
            for s in range(4):
                dve.wait_ge(deg_kept[s], 2 * NB)
            lap.step(dve, dve.tensor_tensor(rdeg, degp[:, 0:NT], degp[:, NT:2 * NT], ALU.add))
            lap.step(dve, dve.tensor_scalar(eq0, rdeg, 0.0, float(ONE8), ALU.is_equal, ALU.mult))
            lap.step(dve, dve.tensor_tensor(rdeg, rdeg, eq0, ALU.add))
            lap.step(dve, dve.tensor_scalar(rdeg, rdeg, X0_SCALE / ONE8, None, ALU.mult))
            dve.reciprocal(rdeg, rdeg).then_inc(rdeg_ready, 1)
            for j in (0, 2):
                dve.wait_ge(agg_ps, 4 + j + 1)
                dve.tensor_copy(aggT[:, 2048 + j * BW:2048 + (j + 1) * BW], ps[:, j, :]).then_inc(agg_kept, 1)
            dve.wait_ge(agg_kept, 8)
            for r in range(NB + 2):
                if r < NB:
                    hb = aggT[:, r * BW:(r + 1) * BW]
                    dve.wait_ge(rb_ps, r + 1)
                    dve.tensor_tensor(hb, hb, ps[:, 2 + r % 2, :], ALU.mult).then_inc(agg_scaled, 1)
                if r >= 2:
                    q = r - 2
                    dve.wait_ge(h_kept, q + 1)
                    last = dve.bn_stats(bstat[:, 6 * q:6 * q + 6], aggT[:, q * BW:(q + 1) * BW])
            lap.step(dve, last)
            dve.bn_aggr(bagg, bstat).then_inc(bvar_ready, 1)

            dve.memset(xp[:, :, 2 * D:PARTS], 1.0)
            dve.wait_ge(xn_in, 16)
            dve.wait_ge(xt_ps, NB)
            for r in range(NB + 1):
                if r < NB:
                    z, stat, mv = node_block(xn, r), (stat4, stat4b)[r % 2], (mv4, mv4b)[r % 2]
                    dve.wait_ge(r_ps, r + 1)
                    dve.tensor_tensor(z, z, ps[:, R_BANKS[r % 4], :].rearrange("p (t d) -> p t d", t=BT),
                                      ALU.add).then_inc(z_ready, 1)
                    dve.wait_ge(z_ready, r + 1)
                    for s in range(BT):
                        last = dve.bn_stats(stat[:, s, :], z[:, s, :])
                    lap.step(dve, last)
                    for s in range(BT):
                        last = dve.bn_aggr(mv[:, s, :], stat[:, s, :])
                    last.then_inc(var_ready, 1)
                if r:
                    q = r - 1
                    z, mv, rs = node_block(xn, q), (mv4, mv4b)[q % 2], (rs4, rs4b)[q % 2]
                    dve.wait_ge(var_ready, q + 1)
                    dve.wait_ge(rstd_ready, q + 1)
                    for s in range(BT):
                        last = dve.tensor_scalar(z[:, s, :], z[:, s, :], mv[:, s, 0:1], rs[:, s:s + 1],
                                                 ALU.subtract, ALU.mult)
                    last.then_inc(xs_ready, 1)

            lap.per, lap.base = 1, lap.n
            with dve.Fori(0, NB) as r:
                lap.start(r)
                v = vp[:, bass.ds(r * BT, BT), :]
                src = ps[:, 2, :].rearrange("p (t d) -> p t d", t=BT)
                dve.wait_ge(vn_ps, r + 1)
                lap.step(dve, dve.tensor_copy(v[:, :, D:2 * D], src))
                dve.tensor_tensor(v[:, :, 0:D], src, v[:, :, D:2 * D], ALU.subtract).then_inc(vn_kept, 1)

            def moments(z, n):
                for s in range(BT):
                    last = dve.bn_stats(stat4[:, s, :], z[:, s, :])
                lap.step(dve, last)
                dve.memset(btmp, 0.0)
                for s in range(BT):
                    last = dve.bn_aggr(mv4[:, s, :], stat4[:, s, :])
                last.then_inc(var_ready, 1)

            def normed(dst, z, n, signal):
                dve.wait_ge(var_ready, n)
                dve.wait_ge(rstd_ready, n)
                for s in range(BT):
                    last = dve.tensor_scalar(dst[:, s, :], z[:, s, :], mv4[:, s, 0:1], rs4[:, s:s + 1],
                                             ALU.subtract, ALU.mult)
                last.then_inc(signal, 1)

            lap.base += NB
            lap.per = 1
            x2s = tmp[1].rearrange("p (t d) -> p t d", t=BT)
            ys = tmp[2].rearrange("p (t d) -> p t d", t=BT)
            def second_block(r, first):
                lap.start(r)
                o = ps[:, 1, :].rearrange("p (t d) -> p t d", t=BT)
                dve.wait_ge(o_ps, r + 1)
                moments(o, 0)
                if not first:
                    dve.wait_ge(x2_high, r)
                    dve.wait_ge(sq_ready, r)
                normed(x2s, o, r + (NB + 1), x2s_ready)
                blk = xp[:, bass.ds(r * BT, BT), :]
                dve.wait_ge(x2_high, r + 1)
                dve.tensor_tensor(blk[:, :, 0:D], x2s, blk[:, :, D:2 * D], ALU.subtract).then_inc(x2_low, 1)
                dve.wait_ge(rn_ready, r + 1)
                if not first:
                    dve.wait_ge(y_ps, r)
                for s in range(BT):
                    last = dve.tensor_scalar(ys[:, s, :], x2s[:, s, :], rn4[:, s:s + 1], None, ALU.mult)
                last.then_inc(y_ready, 1)
                dve.wait_ge(y_high, r + 1)
                yb = yT[:, bass.ds(r, 1), :, :].rearrange("p r h i -> p (r h) i")
                dve.tensor_tensor(yb[:, 1, :], ps[:, 2, :], yb[:, 0, :], ALU.subtract).then_inc(y_kept, 1)

            second_block(0, True)
            with dve.Fori(1, NB) as r:
                second_block(r, False)

            def mask(r, k):
                dve.wait_ge(exp_ready[k % 2], r * (NK // 2) + (k // 2 + 1))
                m = at[:, bass.ds(r * (NK * BW * 2) + k * BW * 2, BW * 2)] if not isinstance(r, int) else \
                    at[:, r * (NK * BW * 2) + k * BW * 2:r * (NK * BW * 2) + (k + 1) * BW * 2]
                e = expo[k % 4].rearrange("p (b i) -> p b i", b=2)
                dve.scalar_tensor_tensor(e, m.rearrange("p (i b) -> p b i", b=2), 0.0, e, ALU.is_gt, ALU.mult
                                         ).then_inc(mask_ready, 1)

            def exp_low(r, k):
                dve.wait_ge(high_ready, r * NK + (k + 1))
                dve.tensor_tensor(elow[k % 4], expo[k % 4], ehigh[k % 4], ALU.subtract).then_inc(low_ready[k % 4], 1)

            def attention_result(r, step):
                if step == 0:
                    dve.wait_ge(num_ready, r + 1)
                    lap.step(dve, dve.reciprocal(va4b, psum_kept[:, :, 2 * D]))
                    for s in range(BT):
                        last = dve.scalar_tensor_tensor(res4[:, s, :], psum_kept[:, s, D:2 * D], va4b[:, s:s + 1],
                                                        res4[:, s, :], ALU.mult, ALU.add)
                    last.then_inc(res_ready, 1)
                if step == 1:
                    dve.wait_ge(res_ready, r + 1)
                    moments(res4, 0)
                if step == 2:
                    normed(x3n[:, bass.ds(r * BT, BT), :] if not isinstance(r, int) else node_block(x3n, r), res4,
                           r + (2 * NB + 1), res_norm)

            def attention_round(r, first):
                for k in range(NK):
                    mask(r, k)
                    if k:
                        exp_low(r, k - 1)
                    elif not first:
                        exp_low(r - 1, NK - 1)
                    if not first and k in (7, 8, 10):
                        attention_result(r - 1, (7, 8, 10).index(k))

            lap.base += NB
            lap.per = 2
            attention_round(0, True)
            with dve.Fori(1, NB) as r:
                lap.start(r - 1)
                attention_round(r, False)
            exp_low(NB - 1, NK - 1)
            dve.wait_ge(w3_in, 48)
            dve.tensor_scalar(w3Ts, w3Ts, HS / S, None, ALU.mult)
            lap_v = Lap(v_lap)
            dve.wait_ge(v_ps, 1)
            lap_v.step(dve, dve.tensor_scalar(vst, ps[:, 5, 0:2], 1.0 / S, None, ALU.mult))
            dve.tensor_copy(vrow, vst[:, 1:2].to_broadcast([P, P])).then_inc(v_ready, 1)
            dve.memset(hx[:, :, D:UW], HS)
            dve.memset(ones_row[0:1, :], 1.0).then_inc(stored, 1)
            lap.start(NB - 1)
            for step in range(3):
                attention_result(NB - 1, step)
            lap.base += 2 * NB
            lap.per, lap.round, lap.n = 0, 0, 0

            dve.wait_ge(st_out, 1)
            dve.tensor_reduce(mx, st[:, :, 0], AX_X, ALU.max).then_inc(mx_ready, 1)
            dve.tensor_scalar(neg_s, st[:, :, 0], -1.0, None, ALU.mult)
            dve.wait_ge(mx_ps, 1)
            dve.tensor_reduce(mxrow[0:1, :], ps[0:1, 0, 0:P], AX_X, ALU.max).then_inc(mx_ready, 1)
            dve.wait_ge(mx_ps, 2)
            dve.tensor_scalar(mall[:, 0:1], ps[:, 1, 0:1], -1.0, None, ALU.mult)
            dve.tensor_scalar(mall[:, 1:2], ps[:, 1, 0:1], -0.2, None, ALU.mult)
            dve.tensor_scalar(mall[:, 2:3], ps[:, 1, 0:1], 0.8, None, ALU.mult).then_inc(mall_ready, 1)
            dve.wait_ge(t_out, 1)

            def u_low_part(n):
                r, g = n // 2, n % 2
                dve.wait_ge(u_high, n + 1)
                dve.tensor_tensor(node_block(ug[g], r)[:, :, 0:UW], uf[g], node_block(ug[g], r)[:, :, UW:2 * UW],
                                  ALU.subtract).then_inc(u_low, 1)

            def codes(r, k):
                if k % 4 == 0:
                    dve.wait_ge(a8_in[k // 4], (r * 16) + 16)
                if not (isinstance(r, int) and r == 0 and k < 4):
                    dve.wait_ge(g1_ready, r * NK + (k - 3))
                    if k % 4 == 3:
                        dve.wait_ge(g2_fourth, r * 4 + k // 4)
                    else:
                        dve.wait_ge(g2_ready, r * 12 + (k // 4 * 3 + k % 4 - 2))
                for u in range(2):
                    t = 2 * k + u
                    a = a8ring[t // 8][:, (t % 8) * BW:(t % 8 + 1) * BW]
                    row = t_row[:, bass.ds(r * BW, BW)] if not isinstance(r, int) else t_row[:, r * BW:(r + 1) * BW]
                    last = dve.scalar_tensor_tensor(code[k % 4][:, u * BW:(u + 1) * BW], row, neg_s[:, t:t + 1], a,
                                                    ALU.is_gt, ALU.add)
                last.then_inc(code_ready, 1)

            def not_positive(r, k, first):
                dve.wait_ge(code_ready, r * NK + (k + 1))
                gate_free(dve, r, k, first)
                dve.tensor_scalar(gate[1][k % 4], code[k % 4], float(ONE8), None, ALU.is_equal).then_inc(g2_ready, 1)

            def gat_result(r, step):
                if step == 0:
                    dve.wait_ge(z_sum, r + 1)
                    lap.step(dve, dve.tensor_scalar(den4, zz[:, :, D], 1.0 / S, None, ALU.mult))
                    lap.step(dve, dve.reciprocal(den4, den4))
                    dve.wait_ge(stored, r * 16 + 1)
                    for s in range(BT):
                        xt = x3n[:, bass.ds(r * BT + s, 1), :].rearrange("p t d -> p (t d)") if not isinstance(r, int) \
                            else x3n[:, r * BT + s, :]
                        last = dve.scalar_tensor_tensor(outs[:, s, :], zz[:, s, 0:D], den4[:, s:s + 1], xt,
                                                        ALU.mult, ALU.add)
                    last.then_inc(zz_ready, 1)
                if step == 1:
                    dve.wait_ge(zz_ready, r + 1)
                    moments(outs, 0)

            def gat_round(r, first):
                for k in range(NK):
                    codes(r, k)
                    if first and k % 2 == 1:
                        for n in (k - 1, k):
                            u_low_part(n)
                    if k % 4:
                        not_positive(r, k - 1, first)
                    if not first and k in (9, 10):
                        gat_result(r - 1, (9, 10).index(k))

            lap.base, lap.per = lap.base, 3
            gat_round(0, True)
            dve.wait_ge(t_out, NB)
            with dve.Fori(1, NB) as r:
                lap.start(r - 1)
                gat_round(r, False)
            lap.start(NB - 1)
            for step in range(2):
                gat_result(NB - 1, step)

        @block.tensor
        def _(pe):
            zeros = zero16[:, :].rearrange("p (o c) -> p o c", o=1).to_broadcast([P, 4, P])
            pe.wait_ge(const_ready, 1)

            def row_products(g, h, first):
                for s in range(4):
                    pe.wait_ge(row_cast[s], g + (h * NB + 1))
                    pe.wait_ge(xs_copied[s], g + (h * NB + 1))
                    if not (first and s < 2):
                        pe.wait_ge(at_written[s % 2], g * 2 + (h * NB * 2 + s // 2))
                    pairs = rows8[s].bitcast(F16)
                    trans = ps[:, 4 + s % 2, :].bitcast(F16)
                    for k in range(HK):
                        last = pe.transpose(trans[:, k * P:(k + 1) * P], pairs[:, k * P:(k + 1) * P], ident16[:, :])
                    last.then_inc(at_ps[s], 1)
                    cols = rows8[s].rearrange("p (j k q b) -> p j k b q", j=4, k=2, b=2)
                    for part in range(2):
                        for j in range(4):
                            last = pe.matmul(ps[:, j, :], xs_tile[:, s, part, :], cols[:, j], start=False, stop=False)
                    last.then_inc(row_used[s], 1)

            for h in range(2):
                if h:
                    pe.wait_ge(agg_kept, 4)
                for j in range(4):
                    pe.matmul(ps[:, j, :], zero16[:, :], zeros, start=True, stop=False)
                if h == 0:
                    row_products(0, 0, True)
                with pe.Fori(1 - h, NB) as g:
                    row_products(g, h, False)
                for j in range(4):
                    pe.matmul(ps[:, j, :], zero16[:, :], zeros, start=False, stop=True).then_inc(agg_ps, 1)
            def inverse_degrees(r):
                for s in range(BT):
                    t = r * BT + s
                    last = pe.matmul(ps[:, 2 + r % 2, s * P:(s + 1) * P], rdeg[:, t:t + 1].to_broadcast([P, P]),
                                     ident[:, :], start=True, stop=True)
                last.then_inc(rb_ps, 1)

            pe.wait_ge(rdeg_ready, 1)
            pe.wait_ge(agg_kept, 8)
            inverse_degrees(0)
            inverse_degrees(1)
            pe.wait_ge(xn_in, 16)
            for r in range(NB + 1):
                if r < NB:
                    if r >= 2:
                        pe.wait_ge(xt_kept, r - 1)
                    for s in range(BT):
                        last = pe.transpose(ps[:, r % 2, s * P:(s + 1) * P], xn[:, r * BT + s, :], ident[:, :])
                    last.then_inc(xt_ps, 1)
                if r:
                    q = r - 1
                    pe.wait_ge(agg_scaled, q + 1)
                    pe.wait_ge(xt_kept, q + 1)
                    if q >= 2:
                        pe.wait_ge(h_kept, q - 1)
                    pe.matmul(ps[:, 4 + q % 2, :], wn_s, aggT[:, q * BW:(q + 1) * BW], start=True, stop=False)
                    pe.matmul(ps[:, 4 + q % 2, :], wc_s, x1T[:, q * BW:(q + 1) * BW], start=False, stop=True
                              ).then_inc(h_ps, 1)
                    if r + 1 < NB:
                        inverse_degrees(r + 1)

            def relu_nodes(r):
                pe.wait_ge(h_relu, r + 1)
                if r >= 4:
                    pe.wait_ge(z_ready, r - 3)
                for s in range(BT):
                    last = pe.transpose(ps[:, R_BANKS[r % 4], s * P:(s + 1) * P],
                                        aggT[:, r * BW + s * P:r * BW + (s + 1) * P], ident[:, :])
                last.then_inc(r_ps, 1)

            def x1_transposed(q):
                pe.wait_ge(xs_ready, q + 1)
                if q >= 2:
                    pe.wait_ge(x1t_kept, q - 1)
                for s in range(BT):
                    last = pe.transpose(ps[:, 4 + q % 2, s * P:(s + 1) * P], xn[:, q * BT + s, :], ident[:, :])
                last.then_inc(x1t_ps, 1)

            def strip_product(r, n, c, parts):
                pe.wait_ge(ring_in[c], r * 16 + (n + 1) * 16)
                if c == 0:
                    if n or not isinstance(r, int):
                        pe.wait_ge(prod_kept, r + n)
                    pe.matmul(ps[:, 0, :], zero16[:, :], zeros, start=True, stop=False)
                else:
                    pe.matmul(ps[:, 0, 0:64], zero16[:, :], zero16[:, 0:64], start=False, stop=False)
                strip = ring[c].rearrange("p (k i b) -> p k b i", k=4, b=2)
                for k in range(4):
                    for b in range(2):
                        t = 2 * (4 * c + k) + b
                        for part in range(2):
                            last_one = c == 3 and k == 3 and b == 1 and part == 1
                            last = pe.matmul(ps[:, 0, :], parts[:, t, part * D:(part + 1) * D], strip[:, k, b, :],
                                             start=False, stop=last_one and n == 0)
                if c < 3:
                    last.then_inc(strip_used[c], 1)
                elif n == 0:
                    last.then_inc(prod_ps, 1)

            def x1_block(r):
                return x1T[:, r * BW:(r + 1) * BW] if isinstance(r, int) else x1T[:, bass.ds(r * BW, BW)]

            def x1_w1(r):
                pe.wait_ge(x1_here, r + 1)
                for s in range(BT):
                    pe.matmul(ps[:, 2, s * P:(s + 1) * P], tmp[1][:, s * P:(s + 1) * P], w_1, start=(s == 0),
                              stop=False)

            def add_t1_w2(r):
                pe.wait_ge(prod_kept, r + 1)
                for s in range(BT):
                    last = pe.matmul(ps[:, 2, s * P:(s + 1) * P], tmp[0][:, s * P:(s + 1) * P], w_2,
                                     start=False, stop=(s == BT - 1))
                last.then_inc(vn_ps, 1)

            def four_transposes(bank, src, signal):
                for s in range(BT):
                    last = pe.transpose(ps[:, bank, s * P:(s + 1) * P], src[:, s * P:(s + 1) * P], ident[:, :])
                last.then_inc(signal, 1)

            for r in range(4):
                relu_nodes(r)
            for q in range(NB):
                x1_transposed(q)
                if q + 4 < NB:
                    relu_nodes(q + 4)
                c = (q - 3) // 2
                if q % 2 and c >= 0:
                    pe.wait_ge(x1_low, 2 * c + 2)
                    strip_product(0, 0, c, xp)
            pe.wait_ge(x1_low, NB)
            strip_product(0, 0, 3, xp)
            x1_w1(0)
            with pe.Fori(1, NB) as r:
                strip_product(r, 0, 0, xp)
                add_t1_w2(r - 1)
                for c in (1, 2, 3):
                    strip_product(r, 0, c, xp)
                x1_w1(r)

            def nodes_out(r):
                pe.wait_ge(prod_kept, r + (NB + 1))
                four_transposes(1, tmp[0], o_ps)

            def cos_operand(r):
                pe.wait_ge(y_ready, r + 1)
                four_transposes(2, tmp[2], y_ps)

            def add_x1(r):
                pe.matmul(ps[:, 0, :], w_b, x1_block(r), start=False, stop=True).then_inc(prod_ps, 1)

            pe.wait_ge(vn_kept, NB - 1)
            strip_product(0, NB, 0, vp)
            add_t1_w2(NB - 1)
            strip_product(0, NB, 1, vp)
            strip_product(0, NB, 2, vp)
            pe.wait_ge(vn_kept, NB)
            strip_product(0, NB, 3, vp)
            add_x1(0)
            with pe.Fori(1, NB) as r:
                strip_product(r, NB, 0, vp)
                nodes_out(r - 1)
                for c in (1, 2, 3):
                    strip_product(r, NB, c, vp)
                add_x1(r)
                cos_operand(r - 1)
            nodes_out(NB - 1)

            def cosines(r, k, first):
                if not (first and k < 2):
                    pe.wait_ge(exp_ready[k % 2], r * (NK // 2) + k // 2)
                def block_part(h):
                    return yT[:, bass.ds(r, 1), h, :].rearrange("p r i -> p (r i)") if not isinstance(r, int) \
                        else yT[:, r, h, :]
                for b in range(2):
                    t = 2 * k + b
                    def tile(h):
                        return yT[:, t // BT, h, (t % BT) * P:(t % BT + 1) * P]
                    bank = ps[:, 4 + 2 * (k % 2) + b, :]
                    pe.matmul(bank, tile(0), block_part(0), start=True, stop=False)
                    pe.matmul(bank, tile(0), block_part(1), start=False, stop=False)
                    last = pe.matmul(bank, tile(1), block_part(0), start=False, stop=True)
                last.then_inc(s_ps[k % 2], 1)

            def weighted_sums(r, k, first):
                pe.wait_ge(low_ready[k % 4], r * 4 + (k // 4 + 1))
                for b in range(2):
                    t = 2 * k + b
                    for s in range(BT):
                        at_ = b * BW + s * P
                        if t == 0 and not first:
                            pe.wait_ge(pv_kept, r * BT + (s + 1 - BT))
                        pe.matmul(ps[:, s, 0:PARTS], ehigh[k % 4][:, at_:at_ + P], xp[:, t, :],
                                  start=(t == 0), stop=False)
                        last = pe.matmul(ps[:, s, D:PARTS], elow[k % 4][:, at_:at_ + P], xp[:, t, D:PARTS],
                                         start=False, stop=(t == NT - 1))
                last.then_inc(pv_done[k % 4], 1)

            def attention_round(r, first):
                for k in range(NK):
                    if not (first and k <= LAG):
                        cosines(r, k, first)
                    if k >= LAG:
                        weighted_sums(r, k - LAG, first)
                    elif not first:
                        weighted_sums(r - 1, NK + k - LAG, first)

            pe.wait_ge(y_kept, NB - 1)
            for k in range(LAG + 1):
                cosines(0, k, True)
            cos_operand(NB - 1)
            pe.wait_ge(y_kept, NB)
            pe.wait_ge(x2_low, NB)
            attention_round(0, True)
            with pe.Fori(1, NB) as r:
                attention_round(r, False)
            pe.wait_ge(w3_in, 48)
            for j in range(2):
                pe.wait_ge(exp_ready[j], NB * NK // 2)
            pe.matmul(ps[:, 5, 0:2], w3s, atts, start=True, stop=True).then_inc(v_ps, 1)
            for k in range(NK - LAG, NK):
                weighted_sums(NB - 1, k, False)

            def features(r):
                if r:
                    pe.wait_ge(h_out, r)
                for s in range(BT):
                    last = pe.matmul(ps[:, H_BANK, s * P:(s + 1) * P],
                                     x3T[:, (r * BT + s) * P:(r * BT + s + 1) * P], w3Ts, start=True, stop=True)
                last.then_inc(h3_ps, 1)

            for r in range(NB + 1):
                if r < NB:
                    if r >= 2:
                        pe.wait_ge(x3t_kept, r - 1)
                    pe.wait_ge(res_norm, r + 1)
                    four_transposes(X3_BANKS[r % 2], x3n[:, r * BT:(r + 1) * BT, :].rearrange("p t d -> p (t d)"),
                                    x3t_ps)
                if r:
                    pe.wait_ge(x3t_kept, r)
                    pe.wait_ge(v_ready, 1)
                    for t in range((r - 1) * BT, r * BT):
                        last = pe.matmul(ps[:, 5, 2 * t:2 * t + 2], x3T[:, t * P:(t + 1) * P], vst,
                                         start=True, stop=True)
                if r == NB:
                    last.then_inc(st_ps, 1)
                if 1 <= r <= EARLY_H:
                    features(r - 1)
            pe.wait_ge(pv_kept, BT * NB)
            for what, r in LATER:
                if what == "h":
                    features(r)
                else:
                    if r == 0:
                        pe.wait_ge(st_out, 1)
                    if r >= 3:
                        pe.wait_ge(t_out, r - 2)
                    pe.matmul(ps[:, T_BANKS[r % 3], :], vrow, x3T[:, r * BW:(r + 1) * BW], start=True, stop=True
                              ).then_inc(t_ps, 1)
                if (what, r) == ("t", 0):
                    pe.wait_ge(mx_ready, 1)
                    pe.transpose(ps[0:1, 0, 0:P], mx, ident[:, :]).then_inc(mx_ps, 1)
                if (what, r) == ("h", EARLY_H):
                    pe.wait_ge(mx_ready, 2)
                    pe.matmul(ps[:, 1, 0:1], ones_row[0:1, :], mxrow[0:1, :], start=True, stop=True
                              ).then_inc(mx_ps, 1)

            def gated_sums(r, k, first):
                if k == 0 and first:
                    pe.wait_ge(h_out, NB)
                    pe.wait_ge(t_out, NB)
                    pe.wait_ge(mall_ready, 1)
                if first:
                    pe.wait_ge(u_low, 2 * (2 * k // BT) + 2)
                pe.wait_ge(g1_ready, r * NK + (k + 1))
                if k % 4 == 3:
                    pe.wait_ge(g2_fourth, r * 4 + (k // 4 + 1))
                else:
                    pe.wait_ge(g2_ready, r * 12 + (k // 4 * 3 + k % 4 + 1))
                pairs = [(u, s, g) for u in range(2) for s in range(BT) for g in range(2)]
                if k == NK - 1:
                    pairs = [(u, s, g) for s in range(BT) for g in range(2) for u in range(2)]
                for u, s, g in pairs:
                    t = 2 * k + u
                    nodes = gate[g][k % 4][:, u * BW:(u + 1) * BW].rearrange("p (k q b) -> p k b q", k=2, b=2)
                    if t == 0 and not first:
                        pe.wait_ge(z_kept, r * 8 + (2 * s + g + 1 - 8))
                    last = pe.matmul(ps[:, 2 * s + g, 0:2 * UW], nodes[:, s // 2, s % 2, :], ug[g][:, t, :],
                                     start=(t == 0), stop=(t == NT - 1))
                    if t == NT - 1:
                        last.then_inc(z_ps, 1)
                if k < NK - 1:
                    last.then_inc(gates_used[k % 4], 1)

            for k in range(NK):
                gated_sums(0, k, True)
            with pe.Fori(1, NB) as r:
                for k in range(NK):
                    gated_sums(r, k, False)


def kernel(**inputs):
    import numpy as _np
    import concourse.bacc as _bacc
    from concourse import mybir as _mybir
    from concourse.bass_utils import run_bass_kernel_spmd as _run

    nc = _bacc.Bacc("TRN2", target_bir_lowering=False, num_devices=1)
    a = {k: _np.asarray(v) for k, v in inputs.items()}
    laid = [("x", a["x"]), ("adj", a["adj"]), ("wnT", a["L0_gnn_W_n"].T), ("wcT", a["L0_gnn_W_c"].T),
            ("bn", a["L0_gnn_b_n"]), ("bc", a["L0_gnn_b_c"]), ("gamma", a["L0_gnn_gamma"]),
            ("beta", a["L0_gnn_beta"]), ("w1", a["L1_gnn_weight"]), ("b1", a["L1_gnn_bias"]),
            ("cos_beta", a["L2_gnn_beta"]), ("w3", a["L3_gnn_weight"]), ("w3T", a["L3_gnn_weight"].T),
            ("att", _np.stack([a["L3_gnn_att_src"][0], a["L3_gnn_att_dst"][0]], axis=1))]
    arrays, args = {}, []
    for name, v in laid:
        arrays[f"in_{name}"] = _np.ascontiguousarray(v)
        args.append(nc.dram_tensor(f"in_{name}", v.shape, _mybir.dt.from_np(v.dtype), kind="ExternalInput").ap())
    args.append(nc.dram_tensor("out_0", (4096, 128), _mybir.dt.float32, kind="ExternalOutput").ap())
    program(nc, *args)
    r = _run(nc, [arrays], core_ids=[0])
    return r.results[0]["out_0"]
```

```python
from contextlib import ExitStack

import concourse.bass as bass
from concourse import mybir

F32 = mybir.dt.float32
F16 = mybir.dt.float16
F8 = mybir.dt.float8e5
U16 = mybir.dt.uint16
U8 = mybir.dt.uint8
ALU = mybir.AluOpType
ACT = mybir.ActivationFunctionType
AX_X = mybir.AxisListType.X

P = 128
N = 4096
D = 128
NT = N // P
BT = 4
NB = NT // BT
BW = BT * P
NK = NT // 2
HK = NK // 2
LN_EPS = 1e-5
COS_EPS = 1e-7
ONE8 = 60
X0_SCALE = 16.0
S = 4096.0
RS = 32768.0
HS = 256.0
PARTS = 2 * D + 1
UW = D + 1
KB = 1024
SMALL = 332


class Lap:

    def __init__(self, sem, per=0, base=0):
        self.sem, self.per, self.base, self.round, self.n = sem, per, base, 0, 0

    def start(self, r):
        self.round, self.n = r, 0

    def done(self, ins):
        ins.then_inc(self.sem, 1)
        self.n += 1

    def wait(self, eng):
        eng.wait_ge(self.sem, self.round * self.per + (self.base + self.n))

    def step(self, eng, ins):
        self.done(ins)
        self.wait(eng)


def program(nc, x, adj, wnT, wcT, bn, bc, gamma, beta, w1, b1, cos_beta, w3, w3T, att, out):
    adj_rows = adj.rearrange("(r k p b) c -> r k b p c", r=NB, k=2, b=2)
    adj_casts = adj.rearrange("(k p b) (i c) -> i b p k c", p=P, b=2, c=BW)
    x_nodes = x.rearrange("(k p b) d -> p k (b d)", p=P, b=2)
    out_nodes = out.rearrange("(r k p b) d -> r p k (b d)", r=NB, k=2, b=2)
    a8_dram = nc.dram_tensor("a8_dram", (P, NB * NT, BW), F8).ap()
    a8_blocks = a8_dram.rearrange("p (i k b) c -> i b p k c", i=NB, b=2)
    a8_strips = a8_dram.rearrange("p (s t) c -> s p (t c)", t=8)

    with ExitStack() as ctx:
        def sb(name, shape, dt):
            return ctx.enter_context(nc.sbuf_tensor(name, shape, dt))

        def sem(name):
            return ctx.enter_context(nc.semaphore(name))

        def sems(name, n):
            return [sem(f"{name}{i}") for i in range(n)]

        at = sb("at", [P, NB * NK * BW * 2], U8)
        work = sb("work", [P, 73984], U8)
        ident = sb("ident", [P, P], F32)
        ident16 = sb("ident16", [P, P], F16)
        weights = sb("weights", [P, 5, D], F32)
        small = sb("small", [P, SMALL], F32)

        ps = ctx.enter_context(nc.psum_tensor("ps", [P, 8, 512], F32))

        def view(a, n, dt):
            return work[:, a:a + n].bitcast(dt)

        LD0, NAT0, XP0, AGG0 = 0, 32 * KB, 40 * KB, 40 * KB + NT * PARTS * 2 + 64
        rows = [view(LD0 + 8 * KB * s, 8 * KB, F32) for s in range(4)]
        rows8 = [view(NAT0 + 2 * KB * s, 2 * KB, F8) for s in range(4)]
        xp = view(XP0, NT * PARTS * 2, F16).rearrange("p (t c) -> p t c", t=NT)
        aggT = view(AGG0, 16 * KB, F32)
        xn = view(0, 16 * KB, F32).rearrange("p (t d) -> p t d", t=NT)
        x1T = view(16 * KB, 16 * KB, F32)
        ring = [view(4 * KB * c, 4 * KB, F8) for c in range(4)]
        vp = view(AGG0, 16 * KB, F16).rearrange("p (t c) -> p t c", t=NT)
        tmp = [view(NAT0 + 2 * KB * s, 2 * KB, F32) for s in range(4)]
        yT = view(16 * KB, 16 * KB, F16).rearrange("p (r h i) -> p r h i", r=NB, h=2)
        small_n = [0]

        def col(n=1):
            a = small_n[0]
            small_n[0] += n
            return small[:, a:a + n]

        bnc, bcc, hbias, gam, bet, b1c, cosb, cscale, cbias = [col() for _ in range(9)]
        deg4 = col(4)
        degp = col(2 * NT)
        rdeg = col(NT)
        eq0 = col(NT)
        rparts = eq0.bitcast(F16)
        bstat = col(NB * 6)
        bagg, bscale, btmp = col(2), col(), col()
        stat4 = col(BT * 6).rearrange("p (t c) -> p t c", t=BT)
        mv4 = col(BT * 2).rearrange("p (t c) -> p t c", t=BT)
        va4, rs4, half4, n24, rn4, va4b, s4, eps4, epss4, epsc4 = [col(BT) for _ in range(10)]
        stat4b = col(BT * 6).rearrange("p (t c) -> p t c", t=BT)
        mv4b = col(BT * 2).rearrange("p (t c) -> p t c", t=BT)
        rs4b, bshift = col(BT), col()
        minus4, nmean4, squares4, minus60, plus1 = col(BT), col(BT), col(BT), col(), col()
        assert small_n[0] <= SMALL
        w_1, w_2, w_b, wn_s, wc_s = [weights[:, j, :] for j in range(5)]

        LAG = 3
        expo = [view(4 * KB * j, 4 * KB, F32) for j in range(4)]
        ehigh = [view(AGG0 + 4 * KB * j, 2 * KB, F16) for j in range(4)]
        elow = [view(AGG0 + 4 * KB * j + 2 * KB, 2 * KB, F16) for j in range(4)]
        psum_kept = view(NAT0, BT * PARTS * 4, F32).rearrange("p (s c) -> p s c", s=BT)
        res4 = view(NAT0 + BT * PARTS * 4 + 16, BT * D * 4, F32).rearrange("p (s d) -> p s d", s=BT)
        place = [0]

        def late(n, dt, size):
            a = place[0]
            place[0] += (n * size + 31) // 32 * 32
            return at[:, a:a + n * size].bitcast(dt)

        x3n = late(NT * D, F32, 4).rearrange("p (t d) -> p t d", t=NT)
        w3s, w3Ts, vrow = late(D, F32, 4), late(D, F32, 4), late(D, F32, 4)
        atts, vst = late(2, F32, 4), late(2, F32, 4)
        assert place[0] <= 32 * KB
        x3T = late(N, F32, 4)
        t_row = late(N, F32, 4)
        hx = late(NT * UW, F32, 4).rearrange("p (t c) -> p t c", t=NT)
        ug = [late(NT * 2 * UW, F16, 2).rearrange("p (t c) -> p t c", t=NT) for _ in range(2)]
        uf = [late(BT * UW, F32, 4).rearrange("p (t c) -> p t c", t=BT) for _ in range(2)]
        zs = late(8 * 2 * UW, F32, 4).rearrange("p (j c) -> p j c", j=8)
        zz = late(BT * UW, F32, 4).rearrange("p (s c) -> p s c", s=BT)
        st = late(2 * NT, F32, 4).rearrange("p (t c) -> p t c", t=NT)
        neg_s, wt1, wt2, rr = late(NT, F32, 4), late(NT, F32, 4), late(NT, F32, 4), late(NT, F32, 4)
        mx, mxrow, mall, ones_row = late(1, F32, 4), late(1, F32, 4), late(4, F32, 4), late(P, F32, 4)
        den4 = late(BT, F32, 4)
        assert place[0] <= 128 * KB
        a8ring = [view(4 * KB * c, 4 * KB, U8) for c in range(4)]
        code = [view(16 * KB + 2 * KB * j, 2 * KB, F16) for j in range(4)]
        gate = [[view((24 + 8 * g) * KB + 2 * KB * j, 2 * KB, F16) for j in range(4)] for g in range(2)]
        outs = view(40 * KB, BT * D * 4, F32).rearrange("p (s d) -> p s d", s=BT)

        const_in, const_ready = sem("const_in"), sem("const_ready")
        x_in, row_in = sems("x_in", 4), sems("row_in", 4)
        x_high, x_low = sem("x_high"), sem("x_low")
        row_cast, deg_kept, xs_copied = sems("row_cast", 4), sems("deg_kept", 4), sems("xs_copied", 4)
        row_used, at_ps, at_written = sems("row_used", 4), sems("at_ps", 4), sems("at_written", 2)
        agg_ps, agg_kept = sem("agg_ps"), sem("agg_kept")
        dve_lap, pool_lap = sem("dve_lap"), sem("pool_lap")
        xn_in, xt_ps, xt_kept = sem("xn_in"), sem("xt_ps"), sem("xt_kept")
        rdeg_ready, rb_ps, agg_scaled = sem("rdeg_ready"), sem("rb_ps"), sem("agg_scaled")
        h_ps, h_kept, h_relu = sem("h_ps"), sem("h_kept"), sem("h_relu")
        bvar_ready, brstd_ready = sem("bvar_ready"), sem("brstd_ready")
        r_ps, z_ready, var_ready, rstd_ready = sem("r_ps"), sem("z_ready"), sem("var_ready"), sem("rstd_ready")
        xs_ready, x1_high, x1_low, x1t_ps, x1t_kept = (sem("xs_ready"), sem("x1_high"), sem("x1_low"),
                                                       sem("x1t_ps"), sem("x1t_kept"))
        ring_in, strip_used = sems("ring_in", 4), sems("strip_used", 3)
        prod_ps, prod_kept = sem("prod_ps"), sem("prod_kept")
        ring_done = strip_used + [prod_ps]
        x1_here, vn_ps, vn_kept = sem("x1_here"), sem("vn_ps"), sem("vn_kept")
        o_ps, x2s_ready, x2_high, x2_low = sem("o_ps"), sem("x2s_ready"), sem("x2_high"), sem("x2_low")
        rn_ready, y_ready, y_ps = sem("rn_ready"), sem("y_ready"), sem("y_ps")
        y_high, y_kept, a8_out = sem("y_high"), sem("y_kept"), sems("a8_out", 2)
        s_ps, exp_ready, mask_ready = sems("s_ps", 2), sems("exp_ready", 2), sem("mask_ready")
        high_ready, low_ready, pv_done = sem("high_ready"), sems("low_ready", 4), sems("pv_done", 4)
        pv_kept, num_ready, res_ready, res_norm = (sem("pv_kept"), sem("num_ready"), sem("res_ready"),
                                                           sem("res_norm"))
        w3_in, v_lap, h3_ps, st_ps, g2_act = sem("w3_in"), sem("v_lap"), sem("h3_ps"), sem("st_ps"), sem("g2_act")
        v_ps, v_ready, x3t_ps, x3t_kept, t_ps = (sem("v_ps"), sem("v_ready"), sem("x3t_ps"), sem("x3t_kept"),
                                                 sem("t_ps"))
        h_out, st_out, t_out, mx_ps, mall_ready, w_ready = (sem("h_out"), sem("st_out"), sem("t_out"), sem("mx_ps"),
                                                            sem("mall_ready"), sem("w_ready"))
        square_ready = sem("square_ready")
        uf_ready, u_high, u_low = sems("uf_ready", 2), sem("u_high"), sem("u_low")
        a8_in, code_ready, g1_ready, g2_ready = sems("a8_in", 4), sem("code_ready"), sem("g1_ready"), sem("g2_ready")
        gates_used, z_ps, z_kept, z_sum = sems("gates_used", 4), sem("z_ps"), sem("z_kept"), sem("z_sum")
        den_ready, z_scaled, zz_ready, out_ready, mx_ready = (sem("den_ready"), sem("z_scaled"), sem("zz_ready"),
                                                              sem("out_ready"), sem("mx_ready"))
        xs_tile = sb("xs_tile", [P, 4, 2, D], F16)
        zero16 = sb("zero16", [P, P], F16)
        stored = sem("stored")

        block = ctx.enter_context(nc.Block())

        def node_block(v, r):
            return v[:, r * BT:(r + 1) * BT, :]

        R_BANKS = (6, 7, 3, 2)

        X3_BANKS, H_BANK, T_BANKS = (4, 6), 7, (5, 4, 6)
        EARLY_H = 5
        LATER = [("t", 0), ("h", 5), ("t", 1), ("h", 6), ("t", 2), ("h", 7)] + [("t", r) for r in range(3, NB)]

        def row_col(v, r, s):
            return v[:, r * BT + s:r * BT + s + 1] if isinstance(r, int) else v[:, bass.ds(r * BT + s, 1)]

        BY_ACT = 4

        def act_steps(k):
            return (k + 8 - BY_ACT) // 8

        def weight_cols(g, r):
            return (wt1, wt2)[g][:, r * BT:(r + 1) * BT].rearrange("p (t o) -> p t o", o=1).to_broadcast([P, BT, UW])

        def gate_free(eng, r, k, first):
            if first and k < 4:
                return
            if k % 4 < 2:
                eng.wait_ge(gates_used[k % 4], r * 4 + k // 4)
            elif k > 3:
                eng.wait_ge(gates_used[k % 4], r * 3 + k // 4)
            elif not first:
                eng.wait_ge(z_ps, r * 8)

        @block.sync
        def _(sp):
            xk = aggT.rearrange("p (k c) -> p k c", k=NK)

            def load_rows(g, h, first):
                for s in range(4):
                    if first:
                        sp.dma_start(xk[:, 4 * s:4 * s + 4, :], x_nodes[:, 4 * s:4 * s + 4, :]).then_inc(x_in[s], 16)
                    else:
                        sp.wait_ge(row_cast[s], g + h * NB)
                    sp.dma_start(rows[s], adj_rows[bass.ds(g, 1), s // 2, s % 2, :, h * 2048:(h + 1) * 2048]
                                 .rearrange("r p c -> (r p) c")).then_inc(row_in[s], 16)

            load_rows(0, 0, True)
            for h in range(2):
                with sp.Fori(1 - h, NB) as g:
                    load_rows(g, h, False)
            for s in range(2):
                sp.wait_ge(row_cast[s], 2 * NB)
            sp.dma_start(xn.rearrange("p (k b) d -> p k (b d)", b=2), x_nodes).then_inc(xn_in, 16)
            for n in range(2):
                if n == 0:
                    for c in range(4):
                        for q in (x1_low, x1_high, x1t_ps):
                            sp.wait_ge(q, 2 * c + 2)
                        sp.dma_start(ring[c].bitcast(U8), at[:, c * 4 * KB:(c + 1) * 4 * KB]
                                     ).then_inc(ring_in[c], 16)
                with sp.Fori(1 - n, NB) as r:
                    for c in range(4):
                        sp.wait_ge(ring_done[c], r + n * NB)
                        sp.dma_start(ring[c].bitcast(U8), at[:, bass.ds((r * 4 + c) * (4 * KB), 4 * KB)]
                                     ).then_inc(ring_in[c], 16)
            sp.wait_ge(mask_ready, (NB - 1) * NK)
            sp.dma_start(w3s, w3).then_inc(w3_in, 16)
            sp.dma_start(w3Ts, w3T).then_inc(w3_in, 16)
            sp.dma_start(atts, att).then_inc(w3_in, 16)
            for q in a8_out:
                sp.wait_ge(q, 16 * NB)
            for j in range(4):
                sp.wait_ge(low_ready[j], NB * 4)
            for r in range(NB + 2):
                for c in range(4 if r < NB else 0):
                    if r:
                        sp.wait_ge(code_ready, r * NK + (4 * c + 4 - NK))
                    sp.dma_start(a8ring[c], a8_strips[r * 4 + c].bitcast(U8)).then_inc(a8_in[c], 16)
                if r >= 2:
                    sp.wait_ge(out_ready, r - 1)
                    sp.dma_start(out_nodes[r - 2], outs.rearrange("p (k b) d -> p k (b d)", k=2)
                                 ).then_inc(stored, 16)
            sp.wait_ge(stored, 16 * NB + 1)

        @block.gpsimd
        def _(pool):
            lap = Lap(pool_lap)
            lap.step(pool, pool.memset(ident[:, :], 0.0))
            lap.step(pool, pool.affine_select(out=ident[:, :], in_=ident[:, :], compare_op=ALU.not_equal, fill=1.0,
                                              base=0, pattern=[[-1, P]], channel_multiplier=1))
            pool.tensor_copy(ident16[:, :], ident[:, :])
            pool.memset(zero16[:, :], 0.0)
            for dst, value in ((s4, S), (eps4, LN_EPS), (epss4, LN_EPS * S * S), (epsc4, COS_EPS),
                               (squares4, D / S ** 2)):
                pool.memset(dst, value)
            pool.memset(minus4, -1.0)
            pool.memset(minus60, -float(ONE8))
            pool.memset(plus1, 1.0)
            pool.memset(half4, -0.5).then_inc(const_ready, 1)

            def inverse_root(dst, value, eps, signal, scale=None):
                lap.step(pool, pool.tensor_tensor(va4, value, eps, ALU.add))
                if scale is None:
                    pool.tensor_tensor(dst, va4, half4, ALU.pow).then_inc(signal, 1)
                else:
                    lap.step(pool, pool.tensor_tensor(dst, va4, half4, ALU.pow))
                    pool.tensor_tensor(dst, dst, scale, ALU.mult).then_inc(signal, 1)

            for dst, src in ((wn_s, wnT), (wc_s, wcT), (w_1, w1[1]), (w_2, w1[2]), (w_b, w1[0])):
                pool.dma_start(dst, src).then_inc(const_in, 16)
            for dst, src in ((bnc, bn), (bcc, bc), (gam, gamma), (bet, beta), (b1c, b1)):
                pool.dma_start(dst, src.rearrange("(p o) -> p o", o=1)).then_inc(const_in, 16)
            pool.dma_start(cosb, cos_beta.rearrange("(p o) -> p o", o=1).to_broadcast([P, 1])
                           ).then_inc(const_in, 16)
            pool.wait_ge(x_low, 1)
            pool.wait_ge(x_high, 1)
            def stationary_copies(g, h, first):
                for s in range(4):
                    if not first:
                        pool.wait_ge(row_used[s], g + h * NB)
                    pool.tensor_copy(xs_tile[:, s, :, :].rearrange("p h d -> p (h d)"),
                                     xp[:, bass.ds(g * BT + s, 1), 0:2 * D].rearrange("p t c -> p (t c)")
                                     ).then_inc(xs_copied[s], 1)
                    pool.wait_ge(row_cast[s], g + (h * NB + 1))
                    pool.tensor_copy(degp[:, bass.ds(g * BT + (h * NT + s), 1)], deg4[:, s:s + 1]
                                     ).then_inc(deg_kept[s], 1)

            stationary_copies(0, 0, True)
            pool.wait_ge(x_low, 4)
            pool.wait_ge(x_high, 4)
            for h in range(2):
                with pool.Fori(1 - h, NB) as g:
                    stationary_copies(g, h, False)
            pool.wait_ge(bvar_ready, 1)
            lap.step(pool, pool.tensor_scalar(bscale, bagg[:, 1:2], LN_EPS, None, ALU.add))
            lap.step(pool, pool.tensor_tensor(bscale, bscale, half4[:, 0:1], ALU.pow))
            lap.step(pool, pool.tensor_tensor(bscale, bscale, gam, ALU.mult))
            lap.step(pool, pool.tensor_tensor(bshift, bagg[:, 0:1], bscale, ALU.mult))
            pool.tensor_tensor(bshift, bet, bshift, ALU.subtract).then_inc(brstd_ready, 1)

            def low(r):
                pool.wait_ge(x1_high, r + 1)
                pool.tensor_tensor(node_block(xp, r)[:, :, 0:D], node_block(xn, r), node_block(xp, r)[:, :, D:2 * D],
                                   ALU.subtract).then_inc(x1_low, 1)

            for r in range(NB):
                pool.wait_ge(var_ready, r + 1)
                inverse_root((rs4, rs4b)[r % 2], (mv4, mv4b)[r % 2][:, :, 1], eps4, rstd_ready, s4)
                if r:
                    low(r - 1)
            low(NB - 1)

            pool.wait_ge(x1t_kept, NB)
            pool.tensor_copy(tmp[1], x1T[:, 0:BW]).then_inc(x1_here, 1)
            with pool.Fori(1, NB) as r:
                pool.wait_ge(vn_kept, r)
                pool.tensor_copy(tmp[1], x1T[:, bass.ds(r * BW, BW)]).then_inc(x1_here, 1)

            for r in range(NB):
                pool.wait_ge(var_ready, NB + r + 1)
                inverse_root(rs4, mv4[:, :, 1], eps4, rstd_ready, s4)
                pool.wait_ge(rstd_ready, NB + r + 1)
                lap.step(pool, pool.tensor_tensor(n24, rs4, rs4, ALU.mult))
                lap.step(pool, pool.tensor_tensor(n24, n24, mv4[:, :, 1], ALU.mult))
                lap.step(pool, pool.tensor_tensor(n24, n24, squares4, ALU.mult))
                inverse_root(rn4, n24, epsc4, rn_ready)

            for r in range(NB):
                for b in range(2):
                    if r:
                        pool.wait_ge(a8_out[b], r * 16)
                    pool.dma_start(a8_blocks[r, b], adj_casts[r, b]).then_inc(a8_out[b], 16)
                if r:
                    pool.wait_ge(res_norm, r)
                else:
                    pool.wait_ge(y_kept, NB)
                    pool.wait_ge(x2_low, NB)
                lap.step(pool, pool.tensor_tensor(res4, node_block(xp, r)[:, :, 0:D],
                                                  node_block(xp, r)[:, :, D:2 * D], ALU.add))
                pool.wait_ge(pv_kept, r * BT + BT)
                pool.tensor_tensor(psum_kept[:, :, D:2 * D], psum_kept[:, :, 0:D], psum_kept[:, :, D:2 * D], ALU.add
                                   ).then_inc(num_ready, 1)
                pool.wait_ge(var_ready, r + (2 * NB + 1))
                inverse_root(rs4, mv4[:, :, 1], epss4, rstd_ready, s4)
            lap.per, lap.base, lap.n = 3, lap.n, 0

            pool.wait_ge(w_ready, 1)

            def weigh(r, g):
                pool.wait_ge(h_out, r + 1)
                pool.wait_ge(u_low, 2 * r + g - 1)
                pool.tensor_tensor(uf[g], node_block(hx, r), weight_cols(g, r), ALU.mult).then_inc(uf_ready[g], 1)

            def block_sums(r):
                pool.wait_ge(z_kept, r * 8 + 8)
                lap.step(pool, pool.tensor_tensor(zs[:, :, 0:UW], zs[:, :, 0:UW], zs[:, :, UW:2 * UW], ALU.add))
                pool.tensor_tensor(zz, zs[:, 0:BT, 0:UW], zs[:, BT:2 * BT, 0:UW], ALU.add).then_inc(z_sum, 1)

            def add_x3(r):
                pool.wait_ge(z_scaled, r + 1)
                pool.tensor_tensor(outs, outs, x3n[:, bass.ds(r * BT, BT), :], ALU.add).then_inc(zz_ready, 1)

            def block_norm(r):
                pool.wait_ge(var_ready, r + (3 * NB + 1))
                pool.tensor_tensor(nmean4, mv4[:, :, 0], minus4, ALU.mult)
                lap.step(pool, pool.tensor_tensor(va4, mv4[:, :, 1], epss4, ALU.add))
                lap.step(pool, pool.tensor_tensor(rs4, va4, half4, ALU.pow))
                pool.tensor_tensor(nmean4, nmean4, rs4, ALU.mult).then_inc(rstd_ready, 1)

            for r in range(1, NB):
                for g in range(2):
                    weigh(r, g)
            with pool.Fori(1, NB) as r:
                lap.start(r - 1)
                block_sums(r - 1)
                add_x3(r - 1)
                block_norm(r - 1)
            lap.start(NB - 1)
            block_norm(NB - 1)

        @block.scalar
        def _(act):
            xf = aggT.rearrange("p (t d) -> p t d", t=NT)

            def x_high_part(c):
                act.wait_ge(x_in[c], 16)
                act.activation(xp[:, c * 8:(c + 1) * 8, D:2 * D], xf[:, c * 8:(c + 1) * 8, :], ACT.Copy,
                               scale=X0_SCALE).then_inc(x_high, 1)

            def cast_rows(g, h, first):
                for s in range(4):
                    if first:
                        x_high_part(s)
                    act.wait_ge(row_in[s], g * 16 + (h * NB + 1) * 16)
                    if not first:
                        act.wait_ge(row_used[s], g + h * NB)
                        act.wait_ge(deg_kept[s], g + h * NB)
                    act.activation(rows8[s].bitcast(U8), rows[s], ACT.Copy, scale=float(ONE8),
                                   accum_out=deg4[:, s:s + 1]).then_inc(row_cast[s], 1)

            cast_rows(0, 0, True)
            for h in range(2):
                with act.Fori(1 - h, NB) as g:
                    cast_rows(g, h, False)
            for j in (1, 3):
                act.wait_ge(agg_ps, 4 + j + 1)
                act.copy(aggT[:, 2048 + j * BW:2048 + (j + 1) * BW], ps[:, j, :]).then_inc(agg_kept, 1)
            for r in range(NB + 1):
                if r < NB:
                    act.wait_ge(xt_ps, r + 1)
                    act.copy(x1T[:, r * BW:(r + 1) * BW], ps[:, 6 + r % 2, :]).then_inc(xt_kept, 1)
                if r:
                    act.wait_ge(h_ps, r)
                    act.activation(aggT[:, (r - 1) * BW:r * BW], ps[:, 4 + (r - 1) % 2, :], ACT.Identity, bias=hbias
                                   ).then_inc(h_kept, 1)

            act.wait_ge(brstd_ready, 1)
            act.wait_ge(h_kept, NB)
            for r in range(NB + 4):
                if r < NB:
                    hb = aggT[:, r * BW:(r + 1) * BW]
                    act.activation(hb, hb, ACT.Relu, bias=bshift, scale=bscale).then_inc(h_relu, 1)
                if 3 <= r < NB + 3:
                    q = r - 3
                    act.wait_ge(xs_ready, q + 1)
                    act.copy(node_block(xp, q)[:, :, D:2 * D], node_block(xn, q)).then_inc(x1_high, 1)
                if r >= 4:
                    q = r - 4
                    act.wait_ge(x1t_ps, q + 1)
                    act.copy(x1T[:, q * BW:(q + 1) * BW], ps[:, 4 + q % 2, :]).then_inc(x1t_kept, 1)

            def first_product(r, first):
                act.wait_ge(prod_ps, r + 1)
                if not first:
                    act.wait_ge(vn_ps, r)
                act.mul(tmp[0], ps[:, 0, :], 1.0 / S).then_inc(prod_kept, 1)

            first_product(0, True)
            with act.Fori(1, NB) as r:
                first_product(r, False)

            def exponentials(r, k, first):
                act.wait_ge(s_ps[k % 2], r * (NK // 2) + (k // 2 + 1))
                if not (first and k < 4):
                    act.wait_ge(low_ready[k % 4], r * 4 + k // 4)
                act.activation(expo[k % 4], ps[:, 4 + 2 * (k % 2):6 + 2 * (k % 2), :].rearrange("p b i -> p (b i)"),
                               ACT.Exp, bias=cbias, scale=cscale).then_inc(exp_ready[k % 2], 1)

            def exp_high(r, k):
                act.wait_ge(mask_ready, r * NK + (k + 1))
                if not (isinstance(r, int) and r == 0 and k < 4):
                    act.wait_ge(pv_done[k % 4], r * 4 + k // 4)
                act.copy(ehigh[k % 4], expo[k % 4]).then_inc(high_ready, 1)

            def second_product(r, first):
                act.wait_ge(prod_ps, r + (NB + 1))
                if not first:
                    act.wait_ge(x2s_ready, r)
                act.activation(tmp[0], ps[:, 0, :], ACT.Identity, bias=b1c).then_inc(prod_kept, 1)
                if not first:
                    cos_high(r - 1)
                if isinstance(r, int) and r == NB - 1:
                    exponentials(0, 0, True)
                    exponentials(0, 1, True)
                act.wait_ge(x2s_ready, r + 1)
                x2s = tmp[1].rearrange("p (t d) -> p t d", t=BT)
                act.copy(xp[:, bass.ds(r * BT, BT), D:2 * D], x2s).then_inc(x2_high, 1)
            def cos_high(r):
                act.wait_ge(y_ps, r + 1)
                act.copy(yT[:, bass.ds(r, 1), 0, :].rearrange("p r i -> p (r i)"), ps[:, 2, :]).then_inc(y_high, 1)

            second_product(0, True)
            with act.Fori(1, NB - 1) as r:
                second_product(r, False)
            second_product(NB - 1, False)
            exp_high(0, 0)
            cos_high(NB - 1)

            def keep_sums(r):
                act.wait_ge(pv_done[(NK - 1) % 4], r * 4 + 4)
                for s in range(BT):
                    act.copy(psum_kept[:, s, :], ps[:, s, 0:PARTS]).then_inc(pv_kept, 1)

            def attention_round(r, first):
                for k in range(NK):
                    if k == LAG and not first:
                        keep_sums(r - 1)
                    if not (first and k < 2):
                        exponentials(r, k, first)
                    if k > (1 if first else 0):
                        exp_high(r, k - 1)
                    elif not first:
                        exp_high(r - 1, NK - 1)

            attention_round(0, True)
            with act.Fori(1, NB) as r:
                attention_round(r, False)
            exp_high(NB - 1, NK - 1)
            keep_sums(NB - 1)

            def keep_h(r):
                act.wait_ge(h3_ps, r + 1)
                act.copy(node_block(hx, r)[:, :, 0:D], ps[:, H_BANK, :].rearrange("p (t d) -> p t d", t=BT)
                         ).then_inc(h_out, 1)

            for r in range(NB + 1):
                if r < NB:
                    act.wait_ge(x3t_ps, r + 1)
                    act.copy(x3T[:, r * BW:(r + 1) * BW], ps[:, X3_BANKS[r % 2], :]).then_inc(x3t_kept, 1)
                if 1 <= r <= EARLY_H:
                    keep_h(r - 1)
            act.wait_ge(st_ps, 1)
            act.copy(st.rearrange("p t c -> p (t c)"), ps[:, 5, 0:2 * NT]).then_inc(st_out, 1)

            def u_high_parts(r):
                for g in range(2):
                    act.wait_ge(uf_ready[g], r + 1)
                    act.copy(node_block(ug[g], r)[:, :, UW:2 * UW], uf[g]).then_inc(u_high, 1)

            def positive(r, k, first):
                act.wait_ge(code_ready, r * NK + (k + 1))
                gate_free(act, r, k, first)
                act.activation(gate[0][k % 4], code[k % 4], ACT.Relu, bias=minus60).then_inc(g1_ready, 1)
                if k % 8 == BY_ACT:
                    act.activation(gate[1][k % 4], code[k % 4], ACT.Square, bias=minus60).then_inc(square_ready, 1)
                    act.wait_ge(square_ready, r * 2 + act_steps(k))
                    act.activation(gate[1][k % 4], gate[1][k % 4], ACT.Relu, bias=plus1, scale=-1.0
                                   ).then_inc(g2_act, 1)

            for what, r in LATER:
                if what == "h":
                    keep_h(r)
                else:
                    act.wait_ge(t_ps, r + 1)
                    act.copy(t_row[:, r * BW:(r + 1) * BW].rearrange("p (k q b) -> p k b q", k=2, b=2),
                             ps[:, T_BANKS[r % 3], :].rearrange("p (k b q) -> p k b q", k=2, b=2)
                             ).then_inc(t_out, 1)
                if (what, r) == ("h", EARLY_H + 1):
                    act.wait_ge(mall_ready, 1)
                    act.activation(wt1, st[:, :, 0], ACT.Exp, bias=mall[:, 0:1])
                    act.activation(wt2, st[:, :, 0], ACT.Exp, bias=mall[:, 1:2], scale=0.2).then_inc(w_ready, 1)
                    act.activation(rr, st[:, :, 1], ACT.Exp, bias=mall[:, 2:3], scale=0.8).then_inc(w_ready, 1)
                if (what, r) == ("t", 3):
                    u_high_parts(0)
                if (what, r) == ("t", 4):
                    positive(0, 0, True)

            def keep_z(r):
                for j in range(8):
                    s, g = j // 2, j % 2
                    act.wait_ge(z_ps, r * 8 + (j + 1))
                    if g:
                        last = act.copy(zs[:, BT + s, :], ps[:, j, 0:2 * UW])
                    else:
                        last = act.mul(zs[:, s, :], ps[:, j, 0:2 * UW], row_col(rr, r, s))
                    last.then_inc(z_kept, 1)

            def block_scaled(r):
                act.wait_ge(den_ready, r + 1)
                act.wait_ge(stored, r * 16 + 1)
                for s in range(BT):
                    last = act.mul(outs[:, s, :], zz[:, s, 0:D], den4[:, s:s + 1])
                last.then_inc(z_scaled, 1)

            def block_out(r):
                act.wait_ge(rstd_ready, r + (3 * NB + 1))
                for s in range(BT):
                    last = act.activation(outs[:, s, :], outs[:, s, :], ACT.Identity, bias=nmean4[:, s:s + 1],
                                          scale=rs4[:, s:s + 1])
                last.then_inc(out_ready, 1)

            def gat_round(r, first):
                for k in range(NK):
                    if first and k and k % 2 == 0:
                        u_high_parts(k // 2)
                    if k == 2 and not first:
                        keep_z(r - 1)
                    if k == 10 and not first:
                        block_scaled(r - 1)
                    if k == 15 and not first:
                        block_out(r - 1)
                    if not (first and k == 0):
                        positive(r, k, first)

            gat_round(0, True)
            with act.Fori(1, NB) as r:
                gat_round(r, False)
            keep_z(NB - 1)
            act.wait_ge(out_ready, NB - 1)
            block_out(NB - 1)

        @block.vector
        def _(dve):
            lap = Lap(dve_lap)
            dve.wait_ge(const_ready, 1)
            xf = aggT.rearrange("p (t d) -> p t d", t=NT)
            def x_low_part(c):
                dve.wait_ge(x_high, c + 1)
                dve.scalar_tensor_tensor(xp[:, c * 8:(c + 1) * 8, 0:D], xf[:, c * 8:(c + 1) * 8, :], X0_SCALE,
                                         xp[:, c * 8:(c + 1) * 8, D:2 * D], ALU.mult, ALU.subtract
                                         ).then_inc(x_low, 1)

            at16 = at[:, :].bitcast(U16)

            def keep_transposed(g, h, first):
                for s in range(4):
                    if first and s < 3:
                        x_low_part(s + 1)
                    dve.wait_ge(at_ps[s], g + (h * NB + 1))
                    src = ps[:, 4 + s % 2, :].bitcast(U16).rearrange("p (k i) -> p k i", k=HK)
                    dst = at16[:, bass.ds(g * (NK * BW) + h * HK * BW, HK * BW)].rearrange(
                        "p (k i) -> p k i", k=HK)[:, :, s * P:(s + 1) * P]
                    dve.tensor_copy(dst, src).then_inc(at_written[s % 2], 1)

            x_low_part(0)
            keep_transposed(0, 0, True)
            dve.wait_ge(const_in, 16 * 11)
            lap.step(dve, dve.tensor_tensor(w_b, w_b, w_2, ALU.subtract))
            lap.step(dve, dve.tensor_tensor(w_b, w_b, ident[:, :], ALU.add))
            dve.tensor_scalar(w_b, w_b, 1.0 / S, None, ALU.mult)
            dve.tensor_scalar(w_1, w_1, 1.0 / S, None, ALU.mult)
            dve.tensor_scalar(w_2, w_2, 2.0, None, ALU.mult)
            dve.tensor_tensor(hbias, bnc, bcc, ALU.add)
            dve.tensor_scalar(cscale, cosb, S ** -2, None, ALU.mult)
            lap.step(dve, dve.tensor_scalar(cbias, cosb, -1.0, None, ALU.mult))
            dve.tensor_tensor(cbias, cosb, cbias, ALU.min).then_inc(const_ready, 1)
            with dve.Fori(1, NB) as g:
                keep_transposed(g, 0, False)
            for j in range(4):
                dve.wait_ge(agg_ps, j + 1)
                dve.tensor_copy(aggT[:, j * BW:(j + 1) * BW], ps[:, j, :]).then_inc(agg_kept, 1)
            with dve.Fori(0, NB) as g:
                keep_transposed(g, 1, False)
            for s in range(4):
                dve.wait_ge(deg_kept[s], 2 * NB)
            lap.step(dve, dve.tensor_tensor(rdeg, degp[:, 0:NT], degp[:, NT:2 * NT], ALU.add))
            lap.step(dve, dve.tensor_scalar(eq0, rdeg, 0.0, float(ONE8), ALU.is_equal, ALU.mult))
            lap.step(dve, dve.tensor_tensor(rdeg, rdeg, eq0, ALU.add))
            lap.step(dve, dve.tensor_scalar(rdeg, rdeg, X0_SCALE / (ONE8 * RS), None, ALU.mult))
            lap.step(dve, dve.reciprocal(rdeg, rdeg))
            lap.step(dve, dve.tensor_copy(rparts[:, 0:NT], rdeg))
            dve.tensor_tensor(rparts[:, NT:2 * NT], rdeg, rparts[:, 0:NT], ALU.subtract).then_inc(rdeg_ready, 1)
            for j in (0, 2):
                dve.wait_ge(agg_ps, 4 + j + 1)
                dve.tensor_copy(aggT[:, 2048 + j * BW:2048 + (j + 1) * BW], ps[:, j, :]).then_inc(agg_kept, 1)
            dve.wait_ge(agg_kept, 8)
            for r in range(NB + 2):
                if r < NB:
                    hb = aggT[:, r * BW:(r + 1) * BW]
                    dve.wait_ge(rb_ps, r + 1)
                    dve.scalar_tensor_tensor(hb, ps[:, 2 + r % 2, :], 1.0 / RS, hb, ALU.mult, ALU.mult
                                             ).then_inc(agg_scaled, 1)
                if r >= 2:
                    q = r - 2
                    dve.wait_ge(h_kept, q + 1)
                    last = dve.bn_stats(bstat[:, 6 * q:6 * q + 6], aggT[:, q * BW:(q + 1) * BW])
            lap.step(dve, last)
            dve.bn_aggr(bagg, bstat).then_inc(bvar_ready, 1)

            dve.memset(xp[:, :, 2 * D:PARTS], 1.0)
            dve.wait_ge(xn_in, 16)
            dve.wait_ge(xt_ps, NB)
            for r in range(NB + 1):
                if r < NB:
                    z, stat, mv = node_block(xn, r), (stat4, stat4b)[r % 2], (mv4, mv4b)[r % 2]
                    dve.wait_ge(r_ps, r + 1)
                    dve.tensor_tensor(z, z, ps[:, R_BANKS[r % 4], :].rearrange("p (t d) -> p t d", t=BT),
                                      ALU.add).then_inc(z_ready, 1)
                    dve.wait_ge(z_ready, r + 1)
                    for s in range(BT):
                        last = dve.bn_stats(stat[:, s, :], z[:, s, :])
                    lap.step(dve, last)
                    for s in range(BT):
                        last = dve.bn_aggr(mv[:, s, :], stat[:, s, :])
                    last.then_inc(var_ready, 1)
                if r:
                    q = r - 1
                    z, mv, rs = node_block(xn, q), (mv4, mv4b)[q % 2], (rs4, rs4b)[q % 2]
                    dve.wait_ge(var_ready, q + 1)
                    dve.wait_ge(rstd_ready, q + 1)
                    for s in range(BT):
                        last = dve.tensor_scalar(z[:, s, :], z[:, s, :], mv[:, s, 0:1], rs[:, s:s + 1],
                                                 ALU.subtract, ALU.mult)
                    last.then_inc(xs_ready, 1)

            lap.per, lap.base = 1, lap.n
            with dve.Fori(0, NB) as r:
                lap.start(r)
                v = vp[:, bass.ds(r * BT, BT), :]
                src = ps[:, 2, :].rearrange("p (t d) -> p t d", t=BT)
                dve.wait_ge(vn_ps, r + 1)
                lap.step(dve, dve.tensor_copy(v[:, :, D:2 * D], src))
                dve.tensor_tensor(v[:, :, 0:D], src, v[:, :, D:2 * D], ALU.subtract).then_inc(vn_kept, 1)

            def moments(z):
                for s in range(BT):
                    last = dve.bn_stats(stat4[:, s, :], z[:, s, :])
                lap.step(dve, last)
                dve.memset(btmp, 0.0)
                for s in range(BT):
                    last = dve.bn_aggr(mv4[:, s, :], stat4[:, s, :])
                last.then_inc(var_ready, 1)

            def normed(dst, z, n, signal):
                dve.wait_ge(var_ready, n)
                dve.wait_ge(rstd_ready, n)
                for s in range(BT):
                    last = dve.tensor_scalar(dst[:, s, :], z[:, s, :], mv4[:, s, 0:1], rs4[:, s:s + 1],
                                             ALU.subtract, ALU.mult)
                last.then_inc(signal, 1)

            lap.base += NB
            lap.per = 1
            x2s = tmp[1].rearrange("p (t d) -> p t d", t=BT)
            ys = tmp[2].rearrange("p (t d) -> p t d", t=BT)

            def mask(r, k):
                dve.wait_ge(exp_ready[k % 2], r * (NK // 2) + (k // 2 + 1))
                m = at[:, bass.ds(r * (NK * BW * 2) + k * BW * 2, BW * 2)] if not isinstance(r, int) else \
                    at[:, r * (NK * BW * 2) + k * BW * 2:r * (NK * BW * 2) + (k + 1) * BW * 2]
                e = expo[k % 4].rearrange("p (b i) -> p b i", b=2)
                dve.scalar_tensor_tensor(e, m.rearrange("p (i b) -> p b i", b=2), 0.0, e, ALU.is_gt, ALU.mult
                                         ).then_inc(mask_ready, 1)

            def exp_low(r, k):
                dve.wait_ge(high_ready, r * NK + (k + 1))
                dve.tensor_tensor(elow[k % 4], expo[k % 4], ehigh[k % 4], ALU.subtract).then_inc(low_ready[k % 4], 1)

            def second_block(r, first, last_block=False):
                lap.start(r)
                o = ps[:, 1, :].rearrange("p (t d) -> p t d", t=BT)
                dve.wait_ge(o_ps, r + 1)
                moments(o)
                if last_block:
                    mask(0, 0)
                if not first:
                    dve.wait_ge(x2_high, r)
                normed(x2s, o, r + (NB + 1), x2s_ready)
                blk = xp[:, bass.ds(r * BT, BT), :]
                dve.wait_ge(x2_high, r + 1)
                dve.tensor_tensor(blk[:, :, 0:D], x2s, blk[:, :, D:2 * D], ALU.subtract).then_inc(x2_low, 1)
                if last_block:
                    mask(0, 1)
                dve.wait_ge(rn_ready, r + 1)
                if not first:
                    dve.wait_ge(y_ps, r)
                for s in range(BT):
                    last = dve.tensor_scalar(ys[:, s, :], x2s[:, s, :], rn4[:, s:s + 1], None, ALU.mult)
                last.then_inc(y_ready, 1)
                if last_block:
                    exp_low(0, 0)
                dve.wait_ge(y_high, r + 1)
                yb = yT[:, bass.ds(r, 1), :, :].rearrange("p r h i -> p (r h) i")
                dve.tensor_tensor(yb[:, 1, :], ps[:, 2, :], yb[:, 0, :], ALU.subtract).then_inc(y_kept, 1)

            second_block(0, True)
            with dve.Fori(1, NB - 1) as r:
                second_block(r, False)
            second_block(NB - 1, False, True)

            def attention_result(r, step):
                if step == 0:
                    dve.wait_ge(num_ready, r + 1)
                    lap.step(dve, dve.reciprocal(va4b, psum_kept[:, :, 2 * D]))
                    for s in range(BT):
                        last = dve.scalar_tensor_tensor(res4[:, s, :], psum_kept[:, s, D:2 * D], va4b[:, s:s + 1],
                                                        res4[:, s, :], ALU.mult, ALU.add)
                    last.then_inc(res_ready, 1)
                if step == 1:
                    dve.wait_ge(res_ready, r + 1)
                    moments(res4)
                if step == 2:
                    normed(x3n[:, bass.ds(r * BT, BT), :] if not isinstance(r, int) else node_block(x3n, r), res4,
                           r + (2 * NB + 1), res_norm)

            def attention_round(r, first):
                for k in range(NK):
                    if not (first and k < 2):
                        mask(r, k)
                    if k > (1 if first else 0):
                        exp_low(r, k - 1)
                    elif not first:
                        exp_low(r - 1, NK - 1)
                    if not first and k in (7, 8, 10):
                        attention_result(r - 1, (7, 8, 10).index(k))

            lap.base += NB
            lap.per = 2
            attention_round(0, True)
            with dve.Fori(1, NB) as r:
                lap.start(r - 1)
                attention_round(r, False)
            exp_low(NB - 1, NK - 1)
            dve.wait_ge(w3_in, 48)
            dve.tensor_scalar(w3Ts, w3Ts, HS / S, None, ALU.mult)
            lap_v = Lap(v_lap)
            dve.wait_ge(v_ps, 1)
            lap_v.step(dve, dve.tensor_scalar(vst, ps[:, 5, 0:2], 1.0 / S, None, ALU.mult))
            dve.tensor_copy(vrow, vst[:, 1:2].to_broadcast([P, P])).then_inc(v_ready, 1)
            dve.memset(hx[:, :, D:UW], HS)
            dve.memset(ones_row[0:1, :], 1.0).then_inc(stored, 1)
            lap.start(NB - 1)
            for step in range(3):
                attention_result(NB - 1, step)
            lap.base += 2 * NB
            lap.per, lap.round, lap.n = 0, 0, 0

            dve.wait_ge(st_out, 1)
            dve.tensor_reduce(mx, st[:, :, 0], AX_X, ALU.max).then_inc(mx_ready, 1)
            dve.tensor_scalar(neg_s, st[:, :, 0], -1.0, None, ALU.mult)
            dve.wait_ge(mx_ps, 1)
            dve.tensor_reduce(mxrow[0:1, :], ps[0:1, 0, 0:P], AX_X, ALU.max).then_inc(mx_ready, 1)
            dve.wait_ge(mx_ps, 2)
            dve.tensor_scalar(mall[:, 0:1], ps[:, 1, 0:1], -1.0, None, ALU.mult)
            dve.tensor_scalar(mall[:, 1:2], ps[:, 1, 0:1], -0.2, None, ALU.mult)
            dve.tensor_scalar(mall[:, 2:3], ps[:, 1, 0:1], 0.8, None, ALU.mult).then_inc(mall_ready, 1)
            dve.wait_ge(t_out, 1)

            def u_low_part(n):
                r, g = n // 2, n % 2
                dve.wait_ge(u_high, n + 1)
                dve.tensor_tensor(node_block(ug[g], r)[:, :, 0:UW], uf[g], node_block(ug[g], r)[:, :, UW:2 * UW],
                                  ALU.subtract).then_inc(u_low, 1)

            def codes(r, k):
                if k % 4 == 0:
                    dve.wait_ge(a8_in[k // 4], (r * 16) + 16)
                if not (isinstance(r, int) and r == 0 and k < 4):
                    dve.wait_ge(g1_ready, r * NK + (k - 3))
                    before = k - 4
                    if before % 8 == BY_ACT:
                        dve.wait_ge(g2_act, r * 2 + act_steps(before))
                    else:
                        dve.wait_ge(g2_ready, r * 14 + (before + 1 - act_steps(before)))
                for u in range(2):
                    t = 2 * k + u
                    a = a8ring[t // 8][:, (t % 8) * BW:(t % 8 + 1) * BW]
                    row = t_row[:, bass.ds(r * BW, BW)] if not isinstance(r, int) else t_row[:, r * BW:(r + 1) * BW]
                    last = dve.scalar_tensor_tensor(code[k % 4][:, u * BW:(u + 1) * BW], row, neg_s[:, t:t + 1], a,
                                                    ALU.is_gt, ALU.add)
                last.then_inc(code_ready, 1)

            def not_positive(r, k, first):
                dve.wait_ge(code_ready, r * NK + (k + 1))
                gate_free(dve, r, k, first)
                dve.tensor_scalar(gate[1][k % 4], code[k % 4], float(ONE8), None, ALU.is_equal).then_inc(g2_ready, 1)

            def inverse_weights(r):
                dve.wait_ge(z_sum, r + 1)
                lap.step(dve, dve.tensor_scalar(den4, zz[:, :, D], 1.0 / S, None, ALU.mult))
                dve.reciprocal(den4, den4).then_inc(den_ready, 1)

            def block_moments(r):
                dve.wait_ge(zz_ready, r + 1)
                moments(outs)

            def gat_round(r, first):
                for k in range(NK):
                    codes(r, k)
                    if first and k == 0:
                        dve.wait_ge(w_ready, 1)
                        dve.wait_ge(h_out, 1)
                        for g in range(2):
                            dve.tensor_tensor(uf[g], node_block(hx, 0), weight_cols(g, 0), ALU.mult
                                              ).then_inc(uf_ready[g], 1)
                    if first and k % 2 == 1:
                        for n in (k - 1, k):
                            u_low_part(n)
                    if k == 0:
                        if not first:
                            not_positive(r - 1, NK - 1, False)
                    elif (k - 1) % 8 != BY_ACT:
                        not_positive(r, k - 1, first)
                    if not first and k == 8:
                        inverse_weights(r - 1)
                    if not first and k == 12:
                        block_moments(r - 1)

            lap.per = 2
            gat_round(0, True)
            dve.wait_ge(t_out, NB)
            with dve.Fori(1, NB) as r:
                lap.start(r - 1)
                gat_round(r, False)
            not_positive(NB - 1, NK - 1, False)
            dve.wait_ge(z_kept, 8 * NB)
            lap_v.step(dve, dve.tensor_tensor(zs[:, :, 0:UW], zs[:, :, 0:UW], zs[:, :, UW:2 * UW], ALU.add))
            dve.tensor_tensor(zz, zs[:, 0:BT, 0:UW], zs[:, BT:2 * BT, 0:UW], ALU.add).then_inc(z_sum, 1)
            lap.start(NB - 1)
            inverse_weights(NB - 1)
            dve.wait_ge(den_ready, NB)
            dve.wait_ge(stored, (NB - 1) * 16 + 1)
            for s in range(BT):
                last = dve.scalar_tensor_tensor(outs[:, s, :], zz[:, s, 0:D], den4[:, s:s + 1],
                                                x3n[:, (NB - 1) * BT + s, :], ALU.mult, ALU.add)
            last.then_inc(zz_ready, 1)
            block_moments(NB - 1)

        @block.tensor
        def _(pe):
            zeros = zero16[:, :].rearrange("p (o c) -> p o c", o=1).to_broadcast([P, 4, P])
            pe.wait_ge(const_ready, 1)

            def row_products(g, h, first):
                for s in range(4):
                    pe.wait_ge(row_cast[s], g + (h * NB + 1))
                    pe.wait_ge(xs_copied[s], g + (h * NB + 1))
                    if not (first and s < 2):
                        pe.wait_ge(at_written[s % 2], g * 2 + (h * NB * 2 + s // 2))
                    pairs = rows8[s].bitcast(F16)
                    trans = ps[:, 4 + s % 2, :].bitcast(F16)
                    for k in range(HK):
                        last = pe.transpose(trans[:, k * P:(k + 1) * P], pairs[:, k * P:(k + 1) * P], ident16[:, :])
                    last.then_inc(at_ps[s], 1)
                    cols = rows8[s].rearrange("p (j k q b) -> p j k b q", j=4, k=2, b=2)
                    for part in range(2):
                        for j in range(4):
                            last = pe.matmul(ps[:, j, :], xs_tile[:, s, part, :], cols[:, j], start=False, stop=False)
                    last.then_inc(row_used[s], 1)

            for h in range(2):
                if h:
                    pe.wait_ge(agg_kept, 4)
                for j in range(4):
                    pe.matmul(ps[:, j, :], zero16[:, :], zeros, start=True, stop=False)
                if h == 0:
                    row_products(0, 0, True)
                with pe.Fori(1 - h, NB) as g:
                    row_products(g, h, False)
                for j in range(4):
                    pe.matmul(ps[:, j, :], zero16[:, :], zeros, start=False, stop=True).then_inc(agg_ps, 1)
            def inverse_degrees(r):
                for s in range(BT):
                    t = r * BT + s
                    for part in range(2):
                        last = pe.matmul(ps[:, 2 + r % 2, s * P:(s + 1) * P],
                                         rparts[:, part * NT + t:part * NT + t + 1].to_broadcast([P, P]),
                                         ident16[:, :], start=(part == 0), stop=(part == 1))
                last.then_inc(rb_ps, 1)

            def x_transposed(r):
                if r >= 2:
                    pe.wait_ge(xt_kept, r - 1)
                for s in range(BT):
                    last = pe.transpose(ps[:, 6 + r % 2, s * P:(s + 1) * P], xn[:, r * BT + s, :], ident[:, :])
                last.then_inc(xt_ps, 1)

            pe.wait_ge(xn_in, 16)
            x_transposed(0)
            x_transposed(1)
            pe.wait_ge(rdeg_ready, 1)
            pe.wait_ge(agg_kept, 8)
            inverse_degrees(0)
            inverse_degrees(1)
            for r in range(NB + 1):
                if 2 <= r < NB:
                    x_transposed(r)
                if r:
                    q = r - 1
                    pe.wait_ge(agg_scaled, q + 1)
                    pe.wait_ge(xt_kept, q + 1)
                    if q >= 2:
                        pe.wait_ge(h_kept, q - 1)
                    pe.matmul(ps[:, 4 + q % 2, :], wn_s, aggT[:, q * BW:(q + 1) * BW], start=True, stop=False)
                    pe.matmul(ps[:, 4 + q % 2, :], wc_s, x1T[:, q * BW:(q + 1) * BW], start=False, stop=True
                              ).then_inc(h_ps, 1)
                    if r + 1 < NB:
                        inverse_degrees(r + 1)

            def relu_nodes(r):
                pe.wait_ge(h_relu, r + 1)
                if r >= 4:
                    pe.wait_ge(z_ready, r - 3)
                for s in range(BT):
                    last = pe.transpose(ps[:, R_BANKS[r % 4], s * P:(s + 1) * P],
                                        aggT[:, r * BW + s * P:r * BW + (s + 1) * P], ident[:, :])
                last.then_inc(r_ps, 1)

            def x1_transposed(q):
                pe.wait_ge(xs_ready, q + 1)
                if q >= 2:
                    pe.wait_ge(x1t_kept, q - 1)
                for s in range(BT):
                    last = pe.transpose(ps[:, 4 + q % 2, s * P:(s + 1) * P], xn[:, q * BT + s, :], ident[:, :])
                last.then_inc(x1t_ps, 1)

            def strip_product(r, n, c, parts):
                pe.wait_ge(ring_in[c], r * 16 + (n + 1) * 16)
                if c == 0:
                    if n or not isinstance(r, int):
                        pe.wait_ge(prod_kept, r + n)
                        pe.matmul(ps[:, 3, 0:64], zero16[:, :], zero16[:, 0:64], start=True, stop=True)
                else:
                    pe.matmul(ps[:, 0, 0:64], zero16[:, :], zero16[:, 0:64], start=False, stop=False)
                strip = ring[c].rearrange("p (k i b) -> p k b i", k=4, b=2)
                for k in range(4):
                    for b in range(2):
                        t = 2 * (4 * c + k) + b
                        for part in range(2):
                            last_one = c == 3 and k == 3 and b == 1 and part == 1
                            last = pe.matmul(ps[:, 0, :], parts[:, t, part * D:(part + 1) * D], strip[:, k, b, :],
                                             start=(t == 0 and part == 0), stop=last_one and n == 0)
                if c < 3:
                    last.then_inc(strip_used[c], 1)
                elif n == 0:
                    last.then_inc(prod_ps, 1)

            def x1_block(r):
                return x1T[:, r * BW:(r + 1) * BW] if isinstance(r, int) else x1T[:, bass.ds(r * BW, BW)]

            def x1_w1(r):
                pe.wait_ge(x1_here, r + 1)
                for s in range(BT):
                    pe.matmul(ps[:, 2, s * P:(s + 1) * P], tmp[1][:, s * P:(s + 1) * P], w_1, start=(s == 0),
                              stop=False)

            def add_t1_w2(r):
                pe.wait_ge(prod_kept, r + 1)
                for s in range(BT):
                    last = pe.matmul(ps[:, 2, s * P:(s + 1) * P], tmp[0][:, s * P:(s + 1) * P], w_2,
                                     start=False, stop=(s == BT - 1))
                last.then_inc(vn_ps, 1)

            def four_transposes(bank, src, signal):
                for s in range(BT):
                    last = pe.transpose(ps[:, bank, s * P:(s + 1) * P], src[:, s * P:(s + 1) * P], ident[:, :])
                last.then_inc(signal, 1)

            for r in range(4):
                relu_nodes(r)
            for q in range(NB):
                x1_transposed(q)
                if q + 4 < NB:
                    relu_nodes(q + 4)
                c = (q - 3) // 2
                if q % 2 and c >= 0:
                    pe.wait_ge(x1_low, 2 * c + 2)
                    strip_product(0, 0, c, xp)
            pe.wait_ge(x1_low, NB)
            strip_product(0, 0, 3, xp)
            x1_w1(0)
            with pe.Fori(1, NB) as r:
                strip_product(r, 0, 0, xp)
                add_t1_w2(r - 1)
                for c in (1, 2, 3):
                    strip_product(r, 0, c, xp)
                x1_w1(r)

            def nodes_out(r):
                pe.wait_ge(prod_kept, r + (NB + 1))
                four_transposes(1, tmp[0], o_ps)

            def cos_operand(r):
                pe.wait_ge(y_ready, r + 1)
                four_transposes(2, tmp[2], y_ps)

            def add_x1(r):
                pe.matmul(ps[:, 0, :], w_b, x1_block(r), start=False, stop=True).then_inc(prod_ps, 1)

            pe.wait_ge(vn_kept, NB - 1)
            strip_product(0, NB, 0, vp)
            add_t1_w2(NB - 1)
            strip_product(0, NB, 1, vp)
            strip_product(0, NB, 2, vp)
            pe.wait_ge(vn_kept, NB)
            strip_product(0, NB, 3, vp)
            add_x1(0)
            with pe.Fori(1, NB) as r:
                strip_product(r, NB, 0, vp)
                nodes_out(r - 1)
                for c in (1, 2, 3):
                    strip_product(r, NB, c, vp)
                add_x1(r)
                cos_operand(r - 1)
            nodes_out(NB - 1)

            def cosines(r, k, first):
                if not (first and k < 2):
                    pe.wait_ge(exp_ready[k % 2], r * (NK // 2) + k // 2)
                def block_part(h):
                    return yT[:, bass.ds(r, 1), h, :].rearrange("p r i -> p (r i)") if not isinstance(r, int) \
                        else yT[:, r, h, :]
                for b in range(2):
                    t = 2 * k + b
                    def tile(h):
                        return yT[:, t // BT, h, (t % BT) * P:(t % BT + 1) * P]
                    bank = ps[:, 4 + 2 * (k % 2) + b, :]
                    pe.matmul(bank, tile(0), block_part(0), start=True, stop=False)
                    pe.matmul(bank, tile(0), block_part(1), start=False, stop=False)
                    last = pe.matmul(bank, tile(1), block_part(0), start=False, stop=True)
                last.then_inc(s_ps[k % 2], 1)

            def weighted_sums(r, k, first):
                pe.wait_ge(low_ready[k % 4], r * 4 + (k // 4 + 1))
                for b in range(2):
                    t = 2 * k + b
                    for s in range(BT):
                        at_ = b * BW + s * P
                        if t == 0 and not first:
                            pe.wait_ge(pv_kept, r * BT + (s + 1 - BT))
                        pe.matmul(ps[:, s, 0:PARTS], ehigh[k % 4][:, at_:at_ + P], xp[:, t, :],
                                  start=(t == 0), stop=False)
                        last = pe.matmul(ps[:, s, D:PARTS], elow[k % 4][:, at_:at_ + P], xp[:, t, D:PARTS],
                                         start=False, stop=(t == NT - 1))
                last.then_inc(pv_done[k % 4], 1)

            def attention_round(r, first):
                for k in range(NK):
                    if not (first and k <= LAG):
                        cosines(r, k, first)
                    if k >= LAG:
                        weighted_sums(r, k - LAG, first)
                    elif not first:
                        weighted_sums(r - 1, NK + k - LAG, first)

            pe.wait_ge(y_kept, NB - 1)
            for k in range(LAG + 1):
                cosines(0, k, True)
            cos_operand(NB - 1)
            pe.wait_ge(y_kept, NB)
            pe.wait_ge(x2_low, NB)
            attention_round(0, True)
            with pe.Fori(1, NB) as r:
                attention_round(r, False)
            pe.wait_ge(w3_in, 48)
            for j in range(2):
                pe.wait_ge(exp_ready[j], NB * NK // 2)
            pe.matmul(ps[:, 5, 0:2], w3s, atts, start=True, stop=True).then_inc(v_ps, 1)
            for k in range(NK - LAG, NK):
                weighted_sums(NB - 1, k, False)

            def features(r):
                if r:
                    pe.wait_ge(h_out, r)
                for s in range(BT):
                    last = pe.matmul(ps[:, H_BANK, s * P:(s + 1) * P],
                                     x3T[:, (r * BT + s) * P:(r * BT + s + 1) * P], w3Ts, start=True, stop=True)
                last.then_inc(h3_ps, 1)

            for r in range(NB + 1):
                if r < NB:
                    if r >= 2:
                        pe.wait_ge(x3t_kept, r - 1)
                    pe.wait_ge(res_norm, r + 1)
                    four_transposes(X3_BANKS[r % 2], x3n[:, r * BT:(r + 1) * BT, :].rearrange("p t d -> p (t d)"),
                                    x3t_ps)
                if r:
                    pe.wait_ge(x3t_kept, r)
                    pe.wait_ge(v_ready, 1)
                    for t in range((r - 1) * BT, r * BT):
                        last = pe.matmul(ps[:, 5, 2 * t:2 * t + 2], x3T[:, t * P:(t + 1) * P], vst,
                                         start=True, stop=True)
                if r == NB:
                    last.then_inc(st_ps, 1)
                if 1 <= r <= EARLY_H:
                    features(r - 1)
            pe.wait_ge(pv_kept, BT * NB)
            for what, r in LATER:
                if what == "h":
                    features(r)
                else:
                    if r == 0:
                        pe.wait_ge(st_out, 1)
                    if r >= 3:
                        pe.wait_ge(t_out, r - 2)
                    pe.matmul(ps[:, T_BANKS[r % 3], :], vrow, x3T[:, r * BW:(r + 1) * BW], start=True, stop=True
                              ).then_inc(t_ps, 1)
                if (what, r) == ("t", 0):
                    pe.wait_ge(mx_ready, 1)
                    pe.transpose(ps[0:1, 0, 0:P], mx, ident[:, :]).then_inc(mx_ps, 1)
                if (what, r) == ("h", EARLY_H):
                    pe.wait_ge(mx_ready, 2)
                    pe.matmul(ps[:, 1, 0:1], ones_row[0:1, :], mxrow[0:1, :], start=True, stop=True
                              ).then_inc(mx_ps, 1)

            def gates_here(r, k, first):
                if k == 0 and first:
                    pe.wait_ge(mall_ready, 1)
                if first:
                    pe.wait_ge(u_low, 2 * (2 * k // BT) + 2)
                pe.wait_ge(g1_ready, r * NK + (k + 1))
                if k % 8 == BY_ACT:
                    pe.wait_ge(g2_act, r * 2 + act_steps(k))
                else:
                    pe.wait_ge(g2_ready, r * 14 + (k + 1 - act_steps(k)))

            def gated_sum(k, u, s, g):
                t = 2 * k + u
                nodes = gate[g][k % 4][:, u * BW:(u + 1) * BW].rearrange("p (k q b) -> p k b q", k=2, b=2)
                return pe.matmul(ps[:, 2 * s + g, 0:2 * UW], nodes[:, s // 2, s % 2, :], ug[g][:, t, :],
                                 start=(t == 0), stop=(t == NT - 1))

            def gat_round(r, first):
                gates_here(r, 0, first)
                for s in range(BT):
                    for g in range(2):
                        if not first:
                            pe.wait_ge(z_kept, r * 8 + (2 * s + g + 1 - 8))
                        elif (s, g) == (2, 0):
                            pe.wait_ge(h_out, NB)
                            pe.wait_ge(t_out, NB)
                        for u in range(2):
                            last = gated_sum(0, u, s, g)
                last.then_inc(gates_used[0], 1)
                for k in range(1, NK - 2):
                    gates_here(r, k, first)
                    for u in range(2):
                        for s in range(BT):
                            for g in range(2):
                                last = gated_sum(k, u, s, g)
                    last.then_inc(gates_used[k % 4], 1)
                gates_here(r, NK - 2, first)
                gates_here(r, NK - 1, first)
                for s in range(BT):
                    for g in range(2):
                        for k in (NK - 2, NK - 1):
                            for u in range(2):
                                last = gated_sum(k, u, s, g)
                        last.then_inc(z_ps, 1)

            gat_round(0, True)
            with pe.Fori(1, NB) as r:
                gat_round(r, False)


def kernel(**inputs):
    import numpy as _np
    import concourse.bacc as _bacc
    from concourse import mybir as _mybir
    from concourse.bass_utils import run_bass_kernel_spmd as _run

    nc = _bacc.Bacc("TRN2", target_bir_lowering=False, num_devices=1)
    a = {k: _np.asarray(v) for k, v in inputs.items()}
    laid = [("x", a["x"]), ("adj", a["adj"]), ("wnT", a["L0_gnn_W_n"].T), ("wcT", a["L0_gnn_W_c"].T),
            ("bn", a["L0_gnn_b_n"]), ("bc", a["L0_gnn_b_c"]), ("gamma", a["L0_gnn_gamma"]),
            ("beta", a["L0_gnn_beta"]), ("w1", a["L1_gnn_weight"]), ("b1", a["L1_gnn_bias"]),
            ("cos_beta", a["L2_gnn_beta"]), ("w3", a["L3_gnn_weight"]), ("w3T", a["L3_gnn_weight"].T),
            ("att", _np.stack([a["L3_gnn_att_src"][0], a["L3_gnn_att_dst"][0]], axis=1))]
    arrays, args = {}, []
    for name, v in laid:
        arrays[f"in_{name}"] = _np.ascontiguousarray(v)
        args.append(nc.dram_tensor(f"in_{name}", v.shape, _mybir.dt.from_np(v.dtype), kind="ExternalInput").ap())
    args.append(nc.dram_tensor("out_0", (4096, 128), _mybir.dt.float32, kind="ExternalOutput").ap())
    program(nc, *args)
    r = _run(nc, [arrays], core_ids=[0])
    return r.results[0]["out_0"]
```
